# Optimizing a Trainium2 kernel written in Bass

```python
import numpy as np
import jax
import jax.numpy as jnp

def _softmax(x, axis=-1):
    return jax.nn.softmax(x, axis=axis)

def _gelu(x):
    return jax.nn.gelu(x, approximate=True)

def _silu(x):
    return jax.nn.silu(x)

def _sigmoid(x):
    return jax.nn.sigmoid(x)

def _layernorm(x, axis=-1, eps=1e-05):
    m = jnp.mean(x, axis=axis, keepdims=True)
    v = jnp.var(x, axis=axis, keepdims=True)
    return (x - m) / jnp.sqrt(v + eps)

def _scatter_add(tgt, idx, src, axis=0):
    return tgt.at[idx].add(src)

def _segment_sum(src, seg, n):
    return jax.ops.segment_sum(src, seg, n)
kernel_name = 'mk_audio_tower_d1_tok_audfeat1024_r4_1b0c00'

def setup_inputs(seed: int=0):
    np.random.seed(seed)
    _w = jnp.asarray

    def _rec_inputs():
        import jax
        import jax.numpy as jnp
        _rk = jax.random.key(seed)
        x = -0.000124254 + 0.999853 * jax.random.normal(jax.random.fold_in(_rk, 1), (16, 375, 256), jnp.float32)
        return x
    x = _rec_inputs()

    def _L0_tok_setup():
        import jax, jax.numpy as jnp
        import numpy as np
        CONTEXT = (-3, 0, 3)
        SUBSAMPLING = 1
        FEAT_DIM = 256
        OUT_DIM = 256
        key = jax.random.key(seed)
        k1, k2, k3 = jax.random.split(key, 3)
        mb, t = (32, 250)
        x = jax.random.normal(k1, (mb, t, FEAT_DIM), dtype=jnp.float32)
        in_dim = FEAT_DIM * len(CONTEXT)
        scale = 1.0 / np.sqrt(in_dim)
        W = jax.random.uniform(k2, (OUT_DIM, in_dim), dtype=jnp.float32, minval=-scale, maxval=scale)
        b = jax.random.uniform(k3, (OUT_DIM,), dtype=jnp.float32, minval=-scale, maxval=scale)
        return {'input': x, 'W': W, 'b': b}
    _L0_tok_all = _L0_tok_setup()
    _L0_tok_in = {k: v for k, v in _L0_tok_all.items() if k in ('W', 'b')}
    del _L0_tok_all

    def _L0_attn_setup():
        import jax, jax.numpy as jnp
        import numpy as np
        DIM = 256
        HID = 384
        K = 4
        N, T = (4, 1024)

        def _mk_forget_base(h, a=0.001, b=0.1, lo=-4.323, hi=-9.0):
            x = np.log(np.expm1(np.linspace(a, b, h, dtype=np.float64)))
            x = (x - x.min()) / (x.max() - x.min())
            x = x * abs(hi - lo) + hi
            return jnp.asarray(x, dtype=jnp.float32)
        key = jax.random.key(seed)
        ks = jax.random.split(key, 6)
        x = jax.random.normal(ks[0], (N, T, DIM), jnp.float32)
        Wi = jax.random.normal(ks[1], (2 * HID, DIM), jnp.float32) * DIM ** (-0.5)
        conv_w = jax.random.normal(ks[2], (HID, 1, K), jnp.float32) * K ** (-0.5)
        conv_b = jax.random.normal(ks[3], (HID,), jnp.float32) * 0.01
        Wg = jax.random.normal(ks[4], (2 * HID, HID), jnp.float32) * HID ** (-0.5)
        bg = jnp.zeros((2 * HID,), jnp.float32)
        forget_base = _mk_forget_base(HID)
        Wo = jax.random.normal(ks[5], (DIM, HID), jnp.float32) * HID ** (-0.5)
        return {'x': x, 'Wi': Wi, 'conv_w': conv_w, 'conv_b': conv_b, 'Wg': Wg, 'bg': bg, 'forget_base': forget_base, 'Wo': Wo}
    _L0_attn_all = _L0_attn_setup()
    _L0_attn_in = {k: v for k, v in _L0_attn_all.items() if k in ('Wi', 'conv_w', 'conv_b', 'Wg', 'bg', 'forget_base', 'Wo')}
    del _L0_attn_all

    def _L0_ffn_setup():
        import jax, jax.numpy as jnp
        import numpy as np

        def _binarize(w):
            alpha = jax.lax.stop_gradient(jnp.mean(jnp.abs(w), axis=1, keepdims=True))
            bw = alpha * jnp.sign(w)
            return w + jax.lax.stop_gradient(bw - w)
        key = jax.random.key(seed)
        k1, k2, k3, k4, k5 = jax.random.split(key, 5)
        D, H = (256, 1024)
        x = jax.random.normal(k1, (64, 196, D), dtype=jnp.float32)
        w1 = jax.random.normal(k2, (H, D), dtype=jnp.float32) * 0.02
        b1 = jax.random.normal(k3, (H,), dtype=jnp.float32) * 0.02
        w2 = jax.random.normal(k4, (D, H), dtype=jnp.float32) * 0.02
        b2 = jax.random.normal(k5, (D,), dtype=jnp.float32) * 0.02
        return {'x': x, 'w1': w1, 'b1': b1, 'w2': w2, 'b2': b2}
    _L0_ffn_all = _L0_ffn_setup()
    _L0_ffn_in = {k: v for k, v in _L0_ffn_all.items() if k in ('w1', 'b1', 'w2', 'b2')}
    del _L0_ffn_all
    return {'x': x, 'L0_tok_W': _L0_tok_in['W'], 'L0_tok_b': _L0_tok_in['b'], 'L0_attn_Wi': _L0_attn_in['Wi'], 'L0_attn_conv_w': _L0_attn_in['conv_w'], 'L0_attn_conv_b': _L0_attn_in['conv_b'], 'L0_attn_Wg': _L0_attn_in['Wg'], 'L0_attn_bg': _L0_attn_in['bg'], 'L0_attn_forget_base': _L0_attn_in['forget_base'], 'L0_attn_Wo': _L0_attn_in['Wo'], 'L0_ffn_w1': _L0_ffn_in['w1'], 'L0_ffn_b1': _L0_ffn_in['b1'], 'L0_ffn_w2': _L0_ffn_in['w2'], 'L0_ffn_b2': _L0_ffn_in['b2']}

def reference(x, L0_tok_W, L0_tok_b, L0_attn_Wi, L0_attn_conv_w, L0_attn_conv_b, L0_attn_Wg, L0_attn_bg, L0_attn_forget_base, L0_attn_Wo, L0_ffn_w1, L0_ffn_b1, L0_ffn_w2, L0_ffn_b2):
    import jax
    import jax.numpy as jnp

    def _L0_tok_ref(input, W, b):
        import jax, jax.numpy as jnp
        import numpy as np
        CONTEXT = (-3, 0, 3)
        SUBSAMPLING = 1
        FEAT_DIM = 256
        OUT_DIM = 256
        mb, t, d = input.shape
        offsets = [c - CONTEXT[0] for c in CONTEXT]
        width = CONTEXT[-1] - CONTEXT[0]
        t_out = (t - width - 1) // SUBSAMPLING + 1
        x = jnp.concatenate([input[:, o:o + (t_out - 1) * SUBSAMPLING + 1:SUBSAMPLING, :] for o in offsets], axis=-1)
        return jnp.einsum('btd,od->bto', x, W) + b

    def _L0_attn_ref(x, Wi, conv_w, conv_b, Wg, bg, forget_base, Wo):
        import jax, jax.numpy as jnp
        import numpy as np
        DIM = 256
        HID = 384
        K = 4
        N, T = (4, 1024)

        def _mk_forget_base(h, a=0.001, b=0.1, lo=-4.323, hi=-9.0):
            x = np.log(np.expm1(np.linspace(a, b, h, dtype=np.float64)))
            x = (x - x.min()) / (x.max() - x.min())
            x = x * abs(hi - lo) + hi
            return jnp.asarray(x, dtype=jnp.float32)
        gi = jnp.einsum('ntc,hc->nth', x, Wi)
        gate, u = jnp.split(gi, 2, axis=-1)
        u = jax.lax.conv_general_dilated(u.transpose(0, 2, 1), conv_w, window_strides=(1,), padding=[(K - 1, 0)], dimension_numbers=('NCH', 'OIH', 'NCH'), feature_group_count=HID) + conv_b[None, :, None]
        u = u.transpose(0, 2, 1)
        fg = jnp.einsum('nth,gh->ntg', u, Wg) + bg
        forget, inp = jnp.split(fg, 2, axis=-1)
        alpha = jnp.exp(-8.0 * jax.nn.softplus(forget_base) * jax.nn.sigmoid(forget))
        beta = jnp.sqrt(1.0 - alpha ** 2 + 1e-06)
        xt = beta * jax.nn.sigmoid(inp) * u

        def step(h, ax):
            a, xx = ax
            h = a * h + xx
            return (h, h)
        _, h = jax.lax.scan(step, jnp.zeros((x.shape[0], HID), x.dtype), (alpha.transpose(1, 0, 2), xt.transpose(1, 0, 2)))
        h = h.transpose(1, 0, 2)
        return jnp.einsum('nth,ch->ntc', jax.nn.gelu(gate, approximate=False) * h, Wo)

    def _L0_ffn_ref(x, w1, b1, w2, b2):
        import jax, jax.numpy as jnp
        import numpy as np

        def _binarize(w):
            alpha = jax.lax.stop_gradient(jnp.mean(jnp.abs(w), axis=1, keepdims=True))
            bw = alpha * jnp.sign(w)
            return w + jax.lax.stop_gradient(bw - w)
        bw1 = _binarize(w1)
        h = jnp.einsum('bsd,hd->bsh', x, bw1) + b1
        h = jax.nn.gelu(h, approximate=False)
        bw2 = _binarize(w2)
        out = jnp.einsum('bsh,dh->bsd', h, bw2) + b2
        return out
    h = _L0_tok_ref(x, L0_tok_W, L0_tok_b)
    h = h + _L0_attn_ref(_layernorm(h, axis=-1), L0_attn_Wi, L0_attn_conv_w, L0_attn_conv_b, L0_attn_Wg, L0_attn_bg, L0_attn_forget_base, L0_attn_Wo)
    h = h + _L0_ffn_ref(_layernorm(h, axis=-1), L0_ffn_w1, L0_ffn_b1, L0_ffn_w2, L0_ffn_b2)
    return h

_drawn_inputs = setup_inputs


def setup_inputs(seed=0):
    import zlib

    import numpy as np

    out = dict(_drawn_inputs(seed))
    spreads = {'L0_attn_bg': (0.0, 0.348)}
    factors = {'L0_ffn_b1': 7.313}
    for name, (base, spread) in spreads.items():
        noise = np.random.default_rng([zlib.crc32(name.encode()), seed]).standard_normal(out[name].shape)
        drawn = base * np.exp(spread * noise) if base else spread * noise
        out[name] = jnp.asarray(drawn.astype(out[name].dtype))
    for name, factor in factors.items():
        out[name] = (out[name] * factor).astype(out[name].dtype)
    return out
```

```python
from contextlib import ExitStack

import concourse.bass as bass
from concourse import mybir

ALU = mybir.AluOpType
ACT = mybir.ActivationFunctionType
F32 = mybir.dt.float32
F32R = mybir.dt.float32r

P = 128
NSEQ = 16
T_IN = 375
DIM = 256
SHIFTS = (0, 3, 6)
T = T_IN - SHIFTS[-1]
TP = T + 1
TT = 123
NT = T // TT
KX = DIM // P
HID = 384
KH = HID // P
FF = 1024
KF = FF // P
PART = ((0, 5), (5, 8))
TAPS = 4
NJ = len(SHIFTS) * KX
LN_EPS = 1e-5
BETA_EPS = 1e-6
GATE_C = -8.0
S_CONVW, S_CONVB, S_BG, S_BASE, S_B1 = 0, 12, 15, 21, 24
S_COLS = 32

BANK_FG = (7, 0, 1, 5, 6, 4)
BANK_T2 = (2, 3)
BANK_TOK = (7, 0, 1)
BANK_E = (5, 6, 4, 2, 3, 1, 5, 6)
BANK_T1 = (7, 0)
BANK_U = (7, 0, 1)
BANK_GATE = (2, 3, 4)
BANK_ATT = (5, 6, 4)
BANK_FFN = 2


def need(eng, sem, value):
    if isinstance(value, int) and value <= 0:
        return
    eng.wait_ge(sem, value)


def at(i, k):
    return isinstance(i, int) and i == k


def tower(nc, xT, wtokT, wiT, wgT, woT, w1T, w2T, params, rows, out):
    with ExitStack() as ctx:
        def sb(name, shape, dt=F32):
            return ctx.enter_context(nc.sbuf_tensor(name, shape, dt))

        def sem(name):
            return ctx.enter_context(nc.semaphore(name))

        ps = ctx.enter_context(nc.psum_tensor("ps", [P, 8, 512], F32))

        tok_wh, tok_wl = sb("tok_wh", [P, NJ, DIM], F32R), sb("tok_wl", [P, NJ, DIM], F32R)
        wi_h, wi_l = sb("wi_h", [P, KX, 2 * HID], F32R), sb("wi_l", [P, KX, 2 * HID], F32R)
        wg_h, wg_l = sb("wg_h", [P, KH, 2 * HID], F32R), sb("wg_l", [P, KH, 2 * HID], F32R)
        wo_h, wo_l = sb("wo_h", [P, KH, DIM], F32R), sb("wo_l", [P, KH, DIM], F32R)
        w1_sign = sb("w1_sign", [P, KX, FF], F32R)
        w2_sign = sb("w2_sign", [P, KF, DIM], F32R)
        stage_a, stage_b = sb("stage_a", [P, 2048]), sb("stage_b", [P, 2048])
        par = sb("par", [P, S_COLS])
        row = sb("row", [P, 2, DIM])
        alpha1 = sb("alpha1", [P, KF])
        alpha2 = sb("alpha2", [P, DIM])
        half_bg = sb("half_bg", [P, 2 * KH])
        decay_c = sb("decay_c", [P, KH])
        sp = sb("sp", [P, 6, KH])
        ident = sb("ident", [P, P])
        ones = sb("ones", [P, P])
        mhalf = sb("mhalf", [P, NT])
        ln_bias = sb("ln_bias", [P, 1])

        x_raw = sb("x_raw", [P, 2, KX, T_IN])
        x_h, x_l = sb("x_h", [P, KX, T_IN], F32R), sb("x_l", [P, KX, T_IN], F32R)
        h = sb("h", [P, 2, NT, DIM])
        outb = sb("outb", [P, 2, NT, DIM])
        ffn_s = sb("ffn_s", [P, NT, DIM])
        xn1, xn2 = sb("xn1", [P, NT, DIM]), sb("xn2", [P, NT, DIM])
        stats = [sb(f"stats{j}", [P, NT, 6]) for j in (0, 1)]
        moment = [sb(f"moment{j}", [P, NT, 5]) for j in (0, 1)]
        mean = [sb(f"mean{j}", [P, NT]) for j in (0, 1)]
        var_eps = [sb(f"var_eps{j}", [P, NT]) for j in (0, 1)]
        rstd = [sb(f"rstd{j}", [P, NT]) for j in (0, 1)]
        xa_h, xa_l = sb("xa_h", [P, KX, TP], F32R), sb("xa_l", [P, KX, TP], F32R)
        xb_h, xb_l = sb("xb_h", [P, KX, TP], F32R), sb("xb_l", [P, KX, TP], F32R)
        uc = sb("uc", [P, KH, T])
        u_h, u_l = sb("u_h", [P, KH, TP], F32R), sb("u_l", [P, KH, TP], F32R)
        gate = sb("gate", [P, 2, KH, T])
        decay = sb("decay", [P, KH, T])
        beta = sb("beta", [P, KH, T])
        state = sb("state", [P, KH, T])
        y_h, y_l = sb("y_h", [P, KH, T], F32R), sb("y_l", [P, KH, T], F32R)
        g = sb("g", [P, KF, T])
        stage_c = g[:, :, :].rearrange("p a b -> p (a b)")[:, 0:KH * 2 * HID]
        g_h, g_l = sb("g_h", [P, KF, T], F32R), sb("g_l", [P, KF, T], F32R)

        in_x = [sem("in_x0"), sem("in_x1")]
        in_tok, in_wi, in_wg, in_wo = sem("in_tok"), sem("in_wi"), sem("in_wg"), sem("in_wo")
        in_w1, in_w2, in_par, in_row = sem("in_w1"), sem("in_w2"), sem("in_par"), sem("in_row")
        out_stored = [sem("out_stored0"), sem("out_stored1")]
        consts_ready, ident_zero, ident_ready, pads_ready = (
            sem("consts_ready"), sem("ident_zero"), sem("ident_ready"), sem("pads_ready"))
        w_hi, w_lo = sem("w_hi"), sem("w_lo")
        sp_step, sp_exp = sem("sp_step"), sem("sp_exp")
        sign_part, signs_ready = sem("sign_part"), sem("signs_ready")
        abs_ready, alpha_sum, alpha_ready = sem("abs_ready"), sem("alpha_sum"), sem("alpha_ready")
        x_hi, x_split = sem("x_hi"), sem("x_split")
        tok_done, h_ready = sem("tok_done"), sem("h_ready")
        bn_ready = [sem("bn_ready1"), sem("bn_ready2")]
        sums_ready, terms_ready = [sem("sums1"), sem("sums2")], [sem("terms1"), sem("terms2")]
        veps_ready, rstd_ready = [sem("veps1"), sem("veps2")], [sem("rstd1"), sem("rstd2")]
        xn1_ready, t1_done, xa_hi, xa_lo = sem("xn1_ready"), sem("t1_done"), sem("xa_hi"), sem("xa_lo")
        gi_done = sem("gi_done")
        tap0_ready, taps, u_hi, u_lo = sem("tap0_ready"), sem("taps"), sem("u_hi"), sem("u_lo")
        gate_ready = sem("gate_ready")
        fg_done, tanh_ready = sem("fg_done"), sem("tanh_ready")
        decay_ready, sq_ready, ln_ready, beta_ready = (
            sem("decay_ready"), sem("sq_ready"), sem("ln_ready"), sem("beta_ready"))
        v_ready, xt_ready, scanned, y_ready, y_hi, y_lo = (
            sem("v_ready"), sem("xt_ready"), sem("scanned"), sem("y_ready"), sem("y_hi"), sem("y_lo"))
        att_done, h2_ready = sem("att_done"), sem("h2_ready")
        xn2_ready, t2_done, xb_hi, xb_lo = sem("xn2_ready"), sem("t2_done"), sem("xb_hi"), sem("xb_lo")
        ff1_done, g_ready, g_hi, g_lo = sem("ff1_done"), sem("g_ready"), sem("g_hi"), sem("g_lo")
        ffn_done, ffn_scaled, outb_ready, out_ready = (
            sem("ffn_done"), sem("ffn_scaled"), sem("outb_ready"), sem("out_ready"))

        def raw(a):
            return a.bitcast(F32)

        def steps(eng, body):
            for i in (0, 1):
                body(i, i % 2)
            with eng.Fori(1, NSEQ // 2 - 1) as pair:
                body(2 * pair, 0)
                body(2 * pair + 1, 1)
            for i in (NSEQ - 2, NSEQ - 1):
                body(i, i % 2)

        def exists(i):
            return not isinstance(i, int) or 0 <= i < NSEQ

        block = ctx.enter_context(nc.Block())

        @block.sync
        def _(sp_eng):
            def load(n, p):
                need(sp_eng, x_split, n - 1)
                sp_eng.dma_start(x_raw[:, p], xT[n]).then_inc(in_x[p], 16)

            def store(n, p):
                need(sp_eng, out_ready, n + 1)
                sp_eng.dma_start(out[n], outb[0:TT, p]).then_inc(out_stored[p], 16)

            load(0, 0)
            sp_eng.dma_start(stage_a[:, 0:NJ * DIM], wtokT).then_inc(in_tok, 16)
            load(1, 1)
            sp_eng.dma_start(stage_c[:, :], wgT).then_inc(in_wg, 16)
            sp_eng.wait_ge(w_hi, 1)
            sp_eng.wait_ge(w_lo, 1)
            sp_eng.dma_start(stage_a[:, :], w1T).then_inc(in_w1, 16)

            def body(i, p):
                if exists(i + 2):
                    load(i + 2, p)
                if exists(i - 1):
                    store(i - 1, 1 - p)

            steps(sp_eng, body)
            store(NSEQ - 1, (NSEQ - 1) % 2)
            for p in (0, 1):
                sp_eng.wait_ge(out_stored[p], 16 * (NSEQ // 2))

        @block.gpsimd
        def _(pool):
            pool.memset(ident[:, :], 0.0).then_inc(ident_zero, 1)
            pool.memset(ones[:, :], 1.0).then_inc(consts_ready, 1)
            pool.memset(mhalf[:, :], -0.5).then_inc(consts_ready, 1)
            pool.memset(ln_bias[:, :], 0.25 * (1.0 + BETA_EPS)).then_inc(consts_ready, 1)
            for padded in (xa_h, xa_l, xb_h, xb_l, u_h, u_l):
                pool.memset(raw(padded[:, :, T:TP]), 0.0).then_inc(pads_ready, 1)
            pool.wait_ge(ident_zero, 1)
            pool.affine_select(out=ident[:, :], in_=ident[:, :], compare_op=ALU.not_equal, fill=1.0, base=0,
                               pattern=[[-1, P]], channel_multiplier=1).then_inc(ident_ready, 1)
            pool.wait_ge(consts_ready, 3)

            def split_x(n, p):
                pool.wait_ge(x_hi, n + 1)
                pool.tensor_tensor(x_l[:, :, :], x_raw[:, p], raw(x_h[:, :, :]), ALU.subtract).then_inc(x_split, 1)

            def rsqrt(n, which):
                pool.wait_ge(veps_ready[which], n + 1)
                pool.tensor_tensor(rstd[which][0:TT, :], var_eps[which][0:TT, :], mhalf[0:TT, :],
                                   ALU.pow).then_inc(rstd_ready[which], 1)

            def body(i, p):
                if exists(i + 1):
                    rsqrt(i + 1, 0)
                if exists(i + 2):
                    split_x(i + 2, p)
                rsqrt(i, 1)
                if not at(i, 0) and not at(i, 1):
                    pool.wait_ge(out_stored[p], 8 * (i - p))
                for t in range(NT):
                    ins = pool.tensor_tensor(outb[0:TT, p, t], h[0:TT, p, t], row[0:TT, 1], ALU.add)
                ins.then_inc(outb_ready, 1)
                if exists(i - 1):
                    finish(i - 1, 1 - p)

            def finish(n, p):
                pool.wait_ge(outb_ready, n + 1)
                pool.wait_ge(ffn_scaled, n + 1)
                pool.tensor_tensor(outb[0:TT, p], outb[0:TT, p], ffn_s[0:TT], ALU.add).then_inc(out_ready, 1)

            split_x(0, 0)
            rsqrt(0, 0)
            split_x(1, 1)
            pool.wait_ge(in_row, 16)
            steps(pool, body)
            finish(NSEQ - 1, (NSEQ - 1) % 2)

        @block.scalar
        def _(act):
            act.dma_start(par[:, :], params).then_inc(in_par, 16)
            act.dma_start(row[:, :, :], rows.partition_broadcast(P)).then_inc(in_row, 16)
            act.dma_start(stage_b[:, 0:KX * 2 * HID], wiT).then_inc(in_wi, 16)

            act.wait_ge(sp_step, 2)
            act.activation(sp[:, 2], sp[:, 1], ACT.Exp, scale=-1.0).then_inc(sp_exp, 1)

            def hi_part(dst, src, arrived):
                act.wait_ge(arrived, 16)
                act.activation(dst, src, ACT.Copy).then_inc(w_hi, 1)

            def x_part(n, p):
                act.wait_ge(in_x[p], 8 * (n - p) + 16)
                need(act, tok_done, 3 * n)
                act.activation(x_h[:, :, :], x_raw[:, p], ACT.Copy).then_inc(x_hi, 1)

            x_part(0, 0)
            hi_part(tok_wh[:, :, :].rearrange("p a b -> p (a b)"), stage_a[:, 0:NJ * DIM], in_tok)
            hi_part(wi_h[:, :, :].rearrange("p a b -> p (a b)"), stage_b[:, 0:KX * 2 * HID], in_wi)
            hi_part(wg_h[:, :, :].rearrange("p a b -> p (a b)"), stage_c[:, :], in_wg)

            def xa_parts(n):
                for c in range(KX):
                    act.wait_ge(t1_done, 2 * n + c + 1)
                    if c == 0:
                        need(act, gi_done, 6 * n)
                    act.activation(xa_h[:, c, 0:T], ps[:, BANK_T1[c], 0:T], ACT.Copy).then_inc(xa_hi, 1)

            def last_tap(n):
                for c in range(KH):
                    act.wait_ge(gi_done, 6 * n + c + 1)
                    if c == 0:
                        need(act, v_ready, n)
                        need(act, u_lo, 3 * n)
                    act.activation(uc[:, c], ps[:, BANK_U[c], 0:T], ACT.Identity,
                                   scale=par[:, S_CONVW + TAPS * c + 3:S_CONVW + TAPS * c + 4],
                                   bias=par[:, S_CONVB + c:S_CONVB + c + 1]).then_inc(tap0_ready, 1)

            def gate_gelu(n, p):
                for c in range(KH):
                    act.wait_ge(gi_done, 6 * n + KH + c + 1)
                    if c == 0:
                        need(act, y_ready, n - 1)
                    act.activation(gate[:, p, c], ps[:, BANK_GATE[c], 0:T], ACT.Gelu).then_inc(gate_ready, 1)

            def u_parts(n):
                need(act, fg_done, 6 * n)
                for c in range(KH):
                    act.wait_ge(taps, 9 * n + 6 + c + 1)
                    act.activation(u_h[:, c, 0:T], uc[:, c], ACT.Copy).then_inc(u_hi, 1)

            def gates_tanh(n):
                for m in range(2 * KH):
                    act.wait_ge(fg_done, 6 * n + m + 1)
                    if m == 0:
                        need(act, scanned, 3 * n)
                    if m == KH:
                        need(act, y_lo, n)
                    dst = decay[:, m] if m < KH else state[:, m - KH]
                    act.activation(dst, ps[:, BANK_FG[m], 0:T], ACT.Tanh, scale=0.5,
                                   bias=half_bg[:, m:m + 1]).then_inc(tanh_ready, 1)

            def xb_parts(n):
                for c in range(KX):
                    act.wait_ge(t2_done, 2 * n + c + 1)
                    if c == 0:
                        need(act, ff1_done, 8 * n)
                    act.activation(xb_h[:, c, 0:T], ps[:, BANK_T2[c], 0:T], ACT.Copy).then_inc(xb_hi, 1)

            def decays(n):
                act.preload_act_table_set("natural_log_exp_and_others")
                for c in range(KH):
                    act.wait_ge(tanh_ready, 6 * n + c + 1)
                    act.activation(decay[:, c], decay[:, c], ACT.Exp, scale=decay_c[:, c:c + 1],
                                   bias=decay_c[:, c:c + 1]).then_inc(decay_ready, 1)
                act.wait_ge(decay_ready, 3 * n + 3)
                need(act, xt_ready, n)
                act.activation(beta[:, :, :], decay[:, :, :], ACT.Square).then_inc(sq_ready, 1)
                act.wait_ge(sq_ready, n + 1)
                act.activation(beta[:, :, :], beta[:, :, :], ACT.Ln, scale=-0.25,
                               bias=ln_bias[:, 0:1]).then_inc(ln_ready, 1)
                act.wait_ge(ln_ready, n + 1)
                act.activation(beta[:, :, :], beta[:, :, :], ACT.Exp, scale=0.5).then_inc(beta_ready, 1)

            def ffn_gelu(n, half):
                for c in range(*PART[half]):
                    act.wait_ge(ff1_done, 8 * n + c + 1)
                    if c == PART[half][0]:
                        need(act, g_lo, 2 * n - 1 + half)
                    act.activation(g[:, c], ps[:, BANK_E[c], 0:T], ACT.Gelu, scale=alpha1[:, c:c + 1],
                                   bias=par[:, S_B1 + c:S_B1 + c + 1]).then_inc(g_ready, 1)

            def ffn_hi(n, half):
                a, b = PART[half]
                act.wait_ge(g_ready, 8 * n + b)
                need(act, ffn_done, n)
                act.activation(g_h[:, a:b], g[:, a:b],
                               ACT.Copy).then_inc(g_hi, 1)

            def y_part(n):
                act.wait_ge(y_ready, n + 1)
                need(act, att_done, 3 * n)
                act.activation(y_h[:, :, :], state[:, :, :], ACT.Copy).then_inc(y_hi, 1)

            act.wait_ge(in_par, 16)
            x_part(1, 1)
            xa_parts(0)
            last_tap(0)
            gate_gelu(0, 0)
            u_parts(0)
            act.wait_ge(w_hi, 3)
            act.wait_ge(w_lo, 3)
            act.dma_start(stage_c[:, 0:KH * DIM], woT).then_inc(in_wo, 16)
            act.dma_start(stage_b[:, :], w2T).then_inc(in_w2, 16)
            act.wait_ge(sp_step, 12)

            def body(i, p):
                gates_tanh(i)
                if exists(i - 1):
                    xb_parts(i - 1)
                decays(i)
                if at(i, 1):
                    act.wait_ge(w_lo, 4)
                if at(i, 0):
                    hi_part(wo_h[:, :, :].rearrange("p a b -> p (a b)"), stage_c[:, 0:KH * DIM], in_wo)
                if exists(i - 1):
                    ffn_gelu(i - 1, 0)
                if exists(i + 1):
                    xa_parts(i + 1)
                if exists(i - 1):
                    ffn_hi(i - 1, 0)
                if exists(i - 1):
                    ffn_gelu(i - 1, 1)
                y_part(i)
                if exists(i + 1):
                    last_tap(i + 1)
                if exists(i - 1):
                    ffn_hi(i - 1, 1)
                if exists(i + 1):
                    gate_gelu(i + 1, 1 - p)
                if exists(i + 2):
                    x_part(i + 2, p)
                if exists(i + 1):
                    u_parts(i + 1)
                if at(i, 0):
                    for k, stage in enumerate((stage_a, stage_b)):
                        act.wait_ge(signs_ready, k + 1)
                        act.activation(stage[:, :], stage[:, :], ACT.Abs).then_inc(abs_ready, 1)
                    act.wait_ge(alpha_ready, 2)

            steps(act, body)
            n = NSEQ - 1
            xb_parts(n)
            for half in (0, 1):
                ffn_gelu(n, half)
                ffn_hi(n, half)

        @block.vector
        def _(dve):
            step = [0]

            def sp_op(ins):
                step[0] += 1
                ins.then_inc(sp_step, 1)
                dve.wait_ge(sp_step, step[0])

            dve.wait_ge(in_par, 16)
            base = par[:, S_BASE:S_BASE + KH]
            sp_op(dve.tensor_scalar(sp[:, 0], base, -1.0, None, ALU.mult))
            sp_op(dve.tensor_tensor(sp[:, 1], base, sp[:, 0], ALU.max))
            sp_op(dve.tensor_scalar(half_bg[:, :], par[:, S_BG:S_BG + 2 * KH], 0.5, None, ALU.mult))
            dve.wait_ge(sp_exp, 1)
            sp_op(dve.tensor_scalar(sp[:, 3], sp[:, 2], 2.0, None, ALU.add))
            sp_op(dve.reciprocal(sp[:, 4], sp[:, 3]))
            sp_op(dve.tensor_tensor(sp[:, 2], sp[:, 2], sp[:, 4], ALU.mult))
            sp_op(dve.tensor_tensor(sp[:, 3], sp[:, 2], sp[:, 2], ALU.mult))
            last = 9
            for k in range(last, 0, -1):
                src = sp[:, 4] if k < last else sp[:, 5]
                if k == last:
                    ins = dve.memset(sp[:, 5], 0.0)
                    ins.then_inc(sp_step, 1)
                    step[0] += 1
                    dve.wait_ge(sp_step, step[0])
                sp_op(dve.scalar_tensor_tensor(out=sp[:, 4], in0=src, scalar=1.0 / (2 * k + 1), in1=sp[:, 3],
                                               op0=ALU.add, op1=ALU.mult))
            sp_op(dve.scalar_tensor_tensor(out=sp[:, 4], in0=sp[:, 4], scalar=1.0, in1=sp[:, 2],
                                           op0=ALU.add, op1=ALU.mult))
            sp_op(dve.tensor_scalar(sp[:, 0], base, 0.0, 0.5 * GATE_C, ALU.max, ALU.mult))
            sp_op(dve.scalar_tensor_tensor(out=decay_c[:, :], in0=sp[:, 4], scalar=GATE_C, in1=sp[:, 0],
                                           op0=ALU.mult, op1=ALU.add))
            assert step[0] >= 12

            def lo_part(k, dst, src, hi):
                dve.wait_ge(w_hi, k)
                dve.tensor_tensor(dst, src, raw(hi), ALU.subtract).then_inc(w_lo, 1)

            def flat(a):
                return a[:, :, :].rearrange("p a b -> p (a b)")

            lo_part(1, flat(tok_wl), stage_a[:, 0:NJ * DIM], flat(tok_wh))
            lo_part(2, flat(wi_l), stage_b[:, 0:KX * 2 * HID], flat(wi_h))

            def signs(k, dst, stage, arrived):
                dve.wait_ge(arrived, 16)
                dve.tensor_scalar(dst, stage, 0.0, None, ALU.is_lt).then_inc(sign_part, 1)
                dve.wait_ge(sign_part, k)
                dve.scalar_tensor_tensor(out=dst, in0=stage, scalar=0.0, in1=raw(dst), op0=ALU.is_gt,
                                         op1=ALU.subtract).then_inc(signs_ready, 1)

            def add_tok(n, p):
                for t in range(NT):
                    dve.wait_ge(tok_done, 3 * n + t + 1)
                    if t == 0:
                        need(dve, outb_ready, n - 1)
                    dve.tensor_tensor(h[0:TT, p, t], ps[0:TT, BANK_TOK[t], 0:DIM], row[0:TT, 0],
                                      ALU.add).then_inc(h_ready, 1)
                    dve.wait_ge(h_ready, 3 * n + t + 1)
                    dve.bn_stats(stats[0][0:TT, t], h[0:TT, p, t]).then_inc(bn_ready[0], 1)
                moments(n, 0)

            def moments(n, which):
                st, mo = stats[which][0:TT], moment[which]
                dve.wait_ge(bn_ready[which], 3 * n + 3)
                dve.tensor_tensor(mo[0:TT, :, 0:2], st[:, :, 1:3], st[:, :, 4:6], ALU.add).then_inc(sums_ready[which], 1)
                dve.tensor_tensor(mo[0:TT, :, 2], st[:, :, 1], st[:, :, 4], ALU.subtract).then_inc(sums_ready[which], 1)
                dve.wait_ge(sums_ready[which], 2 * n + 2)
                dve.tensor_scalar(mo[0:TT, :, 3], mo[0:TT, :, 1], 1.0 / DIM, LN_EPS, ALU.mult,
                                  ALU.add).then_inc(terms_ready[which], 1)
                dve.scalar_tensor_tensor(out=mo[0:TT, :, 4], in0=mo[0:TT, :, 2], scalar=0.25, in1=mo[0:TT, :, 2],
                                         op0=ALU.mult, op1=ALU.mult).then_inc(terms_ready[which], 1)
                dve.tensor_scalar(mean[which][0:TT, :], mo[0:TT, :, 0], 0.5, None, ALU.mult).then_inc(
                    terms_ready[which], 1)
                dve.wait_ge(terms_ready[which], 3 * n + 3)
                dve.tensor_tensor(var_eps[which][0:TT, :], mo[0:TT, :, 3], mo[0:TT, :, 4], ALU.add).then_inc(
                    veps_ready[which], 1)

            def norm(n, p, which, xn, ready, transposed):
                dve.wait_ge(rstd_ready[which], n + 1)
                need(dve, transposed, 2 * n)
                for t in range(NT):
                    dve.tensor_scalar(xn[0:TT, t], h[0:TT, p, t], mean[which][0:TT, t:t + 1],
                                      rstd[which][0:TT, t:t + 1], ALU.subtract, ALU.mult).then_inc(ready, 1)

            def xa_low(n):
                for c in range(KX):
                    dve.wait_ge(xa_hi, 2 * n + c + 1)
                    dve.tensor_tensor(xa_l[:, c, 0:T], ps[:, BANK_T1[c], 0:T], raw(xa_h[:, c, 0:T]),
                                      ALU.subtract).then_inc(xa_lo, 1)

            def conv(n, delays):
                for d in delays:
                    for c in range(KH):
                        if d == 1:
                            dve.wait_ge(tap0_ready, 3 * n + c + 1)
                        else:
                            dve.wait_ge(taps, 9 * n + 3 * (d - 2) + c + 1)
                        w = S_CONVW + TAPS * c + 3 - d
                        dve.scalar_tensor_tensor(out=uc[:, c, d:T], in0=ps[:, BANK_U[c], 0:T - d],
                                                 scalar=par[:, w:w + 1], in1=uc[:, c, d:T],
                                                 op0=ALU.mult, op1=ALU.add).then_inc(taps, 1)

            def u_low(n):
                for c in range(KH):
                    dve.wait_ge(u_hi, 3 * n + c + 1)
                    dve.tensor_tensor(u_l[:, c, 0:T], uc[:, c], raw(u_h[:, c, 0:T]), ALU.subtract).then_inc(u_lo, 1)

            def input_term(n):
                dve.wait_ge(tanh_ready, 6 * n + 6)
                dve.scalar_tensor_tensor(out=state[:, :, :], in0=state[:, :, :], scalar=1.0, in1=uc[:, :, :],
                                         op0=ALU.add, op1=ALU.mult).then_inc(v_ready, 1)

            def xb_low(n):
                for c in range(KX):
                    dve.wait_ge(xb_hi, 2 * n + c + 1)
                    dve.tensor_tensor(xb_l[:, c, 0:T], ps[:, BANK_T2[c], 0:T], raw(xb_h[:, c, 0:T]),
                                      ALU.subtract).then_inc(xb_lo, 1)

            def scale_input(n):
                dve.wait_ge(v_ready, n + 1)
                dve.wait_ge(beta_ready, n + 1)
                dve.tensor_tensor(state[:, :, :], state[:, :, :], beta[:, :, :], ALU.mult).then_inc(xt_ready, 1)

            def recur(n):
                dve.wait_ge(xt_ready, n + 1)
                for c in range(KH):
                    dve.tensor_tensor_scan(state[:, c], decay[:, c], state[:, c], 0.0, ALU.mult,
                                           ALU.add).then_inc(scanned, 1)

            def gated(n, p):
                dve.wait_ge(scanned, 3 * n + 3)
                dve.wait_ge(gate_ready, 3 * n + 3)
                dve.tensor_tensor(state[:, :, :], state[:, :, :], gate[:, p], ALU.mult).then_inc(y_ready, 1)

            def y_low(n):
                dve.wait_ge(y_hi, n + 1)
                dve.tensor_tensor(y_l[:, :, :], state[:, :, :], raw(y_h[:, :, :]), ALU.subtract).then_inc(y_lo, 1)

            def ffn_low(n, half):
                a, b = PART[half]
                dve.wait_ge(g_hi, 2 * n + half + 1)
                dve.tensor_tensor(g_l[:, a:b], g[:, a:b], raw(g_h[:, a:b]), ALU.subtract).then_inc(g_lo, 1)

            def add_att(n, p):
                for t in range(NT):
                    dve.wait_ge(att_done, 3 * n + t + 1)
                    dve.tensor_tensor(h[0:TT, p, t], h[0:TT, p, t], ps[0:TT, BANK_ATT[t], 0:DIM],
                                      ALU.add).then_inc(h2_ready, 1)
                for t in range(NT):
                    dve.wait_ge(h2_ready, 3 * n + t + 1)
                    dve.bn_stats(stats[1][0:TT, t], h[0:TT, p, t]).then_inc(bn_ready[1], 1)
                moments(n, 1)

            def scale_ffn(n):
                dve.wait_ge(ffn_done, n + 1)
                need(dve, out_ready, n)
                prod = ps[0:TT, BANK_FFN:BANK_FFN + 2].rearrange("p b n -> p (b n)")
                for t in range(NT):
                    ins = dve.tensor_tensor(ffn_s[0:TT, t], prod[:, t * DIM:(t + 1) * DIM], alpha2[0:TT, :],
                                            ALU.mult)
                ins.then_inc(ffn_scaled, 1)

            dve.wait_ge(in_row, 16)
            add_tok(0, 0)
            norm(0, 0, 0, xn1, xn1_ready, t1_done)
            xa_low(0)
            lo_part(3, flat(wg_l), stage_c[:, :], flat(wg_h))
            conv(0, (1, 2, 3))
            u_low(0)

            def body(i, p):
                if at(i, 0):
                    signs(1, flat(w1_sign), stage_a[:, :], in_w1)
                input_term(i)
                if exists(i - 1):
                    xb_low(i - 1)
                if exists(i + 1):
                    add_tok(i + 1, 1 - p)
                scale_input(i)
                if exists(i + 1):
                    norm(i + 1, 1 - p, 0, xn1, xn1_ready, t1_done)
                recur(i)
                if exists(i + 1):
                    xa_low(i + 1)
                gated(i, p)
                if exists(i - 1):
                    ffn_low(i - 1, 0)
                if at(i, 0):
                    lo_part(4, flat(wo_l), stage_c[:, 0:KH * DIM], flat(wo_h))
                y_low(i)
                if exists(i + 1):
                    conv(i + 1, (1,))
                if exists(i - 1):
                    ffn_low(i - 1, 1)
                if exists(i + 1):
                    conv(i + 1, (2, 3))
                    u_low(i + 1)
                if at(i, 0):
                    signs(2, flat(w2_sign), stage_b[:, :], in_w2)
                add_att(i, p)
                norm(i, p, 1, xn2, xn2_ready, t2_done)
                if exists(i - 1):
                    scale_ffn(i - 1)
                if at(i, 0):
                    dve.wait_ge(alpha_sum, 1)
                    dve.tensor_scalar(alpha1[:, :], ps[:, 2, 0:2 * KF:2], 1.0 / DIM, None,
                                      ALU.mult).then_inc(alpha_ready, 1)
                    dve.wait_ge(alpha_sum, 2)
                    dve.tensor_scalar(alpha2[:, :], ps[:, 3, 0:DIM], 1.0 / FF, None, ALU.mult).then_inc(alpha_ready, 1)

            steps(dve, body)
            n = NSEQ - 1
            xb_low(n)
            ffn_low(n, 0)
            ffn_low(n, 1)
            scale_ffn(n)

        @block.tensor
        def _(pe):
            def split_product(acc, pairs, first=True, last=True):
                for k, (a, b) in enumerate(pairs):
                    ins = pe.matmul(acc, a, b, start=(first and k == 0), stop=(last and k == len(pairs) - 1))
                return ins

            def A(n):
                pe.wait_ge(x_split, n + 1)
                for t in range(NT):
                    need(pe, tanh_ready, 6 * (n - 1) + t + 1)
                    pairs = []
                    for j in range(NJ):
                        f0 = t * TT + SHIFTS[j // KX]
                        xh, xl = (x[:, j % KX, f0:f0 + TT] for x in (x_h, x_l))
                        pairs += [(xh, tok_wh[:, j]), (xh, tok_wl[:, j]), (xl, tok_wh[:, j])]
                    split_product(ps[0:TT, BANK_TOK[t], 0:DIM], pairs).then_inc(tok_done, 1)

            def transposes(n, xn, ready, banks, done):
                for t in range(NT):
                    pe.wait_ge(ready, 3 * n + t + 1)
                    for c in range(KX):
                        ins = pe.transpose(ps[:, banks[c], t * TT:(t + 1) * TT], xn[0:TT, t, c * P:(c + 1) * P],
                                           ident[0:TT, 0:TT])
                        if t == NT - 1:
                            ins.then_inc(done, 1)

            def B(n, prev):
                for m in range(2 * KH):
                    held = {2: 5, 3: 3, 4: 4, 5: 2}
                    if exists(prev) and m in held:
                        pe.wait_ge(g_ready, 8 * prev + held[m] + 1)
                    if at(n, 1) and m in (2, 5):
                        pe.wait_ge(tanh_ready, m + 1)
                    bank = BANK_U[m] if m < KH else BANK_GATE[m - KH]
                    f0 = HID + m * P if m < KH else (m - KH) * P
                    for k in range(KX):
                        wh, wl = wi_h[:, k, f0:f0 + P], wi_l[:, k, f0:f0 + P]
                        if m == 0:
                            pe.wait_ge(xa_lo, 2 * n + k + 1)
                        ins = split_product(ps[:, bank, 0:TP], [(wh, xa_h[:, k]), (wl, xa_h[:, k]), (wh, xa_l[:, k])],
                                            k == 0, k == KX - 1)
                    ins.then_inc(gi_done, 1)

            def C(n):
                for m in range(2 * KH):
                    if m >= KH:
                        need(pe, h2_ready, 3 * (n - 1) + (m - KH) + 1)
                    for k in range(KH):
                        wh, wl = wg_h[:, k, m * P:(m + 1) * P], wg_l[:, k, m * P:(m + 1) * P]
                        if m == 0:
                            pe.wait_ge(u_lo, 3 * n + k + 1)
                        ins = split_product(ps[:, BANK_FG[m], 0:TP], [(wh, u_h[:, k]), (wl, u_h[:, k]), (wh, u_l[:, k])],
                                            k == 0, k == KH - 1)
                    ins.then_inc(fg_done, 1)

            def D(n, prev):
                pe.wait_ge(y_lo, n + 1)
                for t in range(NT):
                    if exists(prev) and t < 2:
                        pe.wait_ge(g_ready, 8 * prev + 7 + t)
                    if exists(n + 1) and t == 2:
                        pe.wait_ge(gate_ready, 3 * (n + 1) + 3)
                    pairs = []
                    for k in range(KH):
                        yh, yl = (y[:, k, t * TT:(t + 1) * TT] for y in (y_h, y_l))
                        pairs += [(yh, wo_h[:, k]), (yh, wo_l[:, k]), (yl, wo_h[:, k])]
                    split_product(ps[0:TT, BANK_ATT[t], 0:DIM], pairs).then_inc(att_done, 1)

            def E(n, half):
                for c in range(*PART[half]):
                    if c == 0:
                        pe.wait_ge(xb_lo, 2 * n + 2)
                    if c < 3 and exists(n + 1):
                        pe.wait_ge(tanh_ready, 6 * (n + 1) + 4 + c)
                    if c >= 6:
                        pe.wait_ge(g_ready, 8 * n + c - 5)
                    pairs = []
                    for k in range(KX):
                        w = w1_sign[:, k, c * P:(c + 1) * P]
                        pairs += [(w, xb_h[:, k]), (w, xb_l[:, k])]
                    split_product(ps[:, BANK_E[c], 0:TP], pairs).then_inc(ff1_done, 1)

            def F(n):
                pe.wait_ge(g_lo, 2 * n + 2)
                if exists(n + 2):
                    pe.wait_ge(gate_ready, 3 * (n + 2) + 2)
                prod = ps[0:TT, BANK_FFN:BANK_FFN + 2].rearrange("p b n -> p (b n)")
                for t in range(NT):
                    pairs = []
                    for c in range(KF):
                        pairs += [(gp[:, c, t * TT:(t + 1) * TT], w2_sign[:, c]) for gp in (g_h, g_l)]
                    ins = split_product(prod[:, t * DIM:(t + 1) * DIM], pairs)
                ins.then_inc(ffn_done, 1)

            pe.wait_ge(w_lo, 1)
            A(0)
            pe.wait_ge(ident_ready, 1)
            transposes(0, xn1, xn1_ready, BANK_T1, t1_done)
            pe.wait_ge(w_lo, 2)
            pe.wait_ge(pads_ready, 6)
            B(0, -1)
            pe.wait_ge(w_lo, 3)

            def body(i, p):
                C(i)
                if exists(i - 1):
                    need(pe, ffn_scaled, i - 1)
                    if at(i, 1):
                        pe.wait_ge(alpha_ready, 2)
                    transposes(i - 1, xn2, xn2_ready, BANK_T2, t2_done)
                if exists(i + 1):
                    A(i + 1)
                if exists(i - 1):
                    E(i - 1, 0)
                if exists(i + 1):
                    transposes(i + 1, xn1, xn1_ready, BANK_T1, t1_done)
                if exists(i - 1):
                    E(i - 1, 1)
                if exists(i + 1):
                    B(i + 1, i - 1)
                if at(i, 0):
                    pe.wait_ge(w_lo, 4)
                D(i, i - 1)
                if exists(i - 1):
                    F(i - 1)
                if at(i, 0):
                    pe.wait_ge(gate_ready, 5)
                    pe.wait_ge(consts_ready, 3)
                    for c in range(KF):
                        if c == 0:
                            pe.wait_ge(abs_ready, 1)
                        for k in range(KX):
                            ins = pe.matmul(ps[:, 2, 2 * c:2 * c + 2],
                                            stage_a[:, k * FF + c * P:k * FF + (c + 1) * P], ones[:, 0:2],
                                            start=(k == 0), stop=(k == KX - 1))
                    ins.then_inc(alpha_sum, 1)
                    pe.wait_ge(abs_ready, 2)
                    for c in range(KF):
                        ins = pe.matmul(ps[:, 3, 0:DIM], ones[:, :], stage_b[:, c * DIM:(c + 1) * DIM],
                                        start=(c == 0), stop=(c == KF - 1))
                    ins.then_inc(alpha_sum, 1)

            steps(pe, body)
            n = NSEQ - 1
            need(pe, ffn_scaled, n)
            transposes(n, xn2, xn2_ready, BANK_T2, t2_done)
            E(n, 0)
            E(n, 1)
            F(n)


def chunked(a, k):
    import numpy as np
    return np.ascontiguousarray(a.reshape(k, P, a.shape[1]).transpose(1, 0, 2).reshape(P, k * a.shape[1]))


def kernel(x, L0_tok_W, L0_tok_b, L0_attn_Wi, L0_attn_conv_w, L0_attn_conv_b, L0_attn_Wg, L0_attn_bg,
           L0_attn_forget_base, L0_attn_Wo, L0_ffn_w1, L0_ffn_b1, L0_ffn_w2, L0_ffn_b2):
    import numpy as np
    import concourse.bacc as bacc
    from concourse.bass_utils import run_bass_kernel_spmd

    def cols(v):
        return np.asarray(v).reshape(-1, P).T

    conv_w = np.asarray(L0_attn_conv_w).reshape(KH, P, TAPS).transpose(1, 0, 2).reshape(P, KH * TAPS)
    arrays = {
        "xT": np.ascontiguousarray(np.asarray(x).reshape(NSEQ, T_IN, KX, P).transpose(0, 3, 2, 1)),
        "wtokT": chunked(np.asarray(L0_tok_W).T, NJ),
        "wiT": chunked(np.asarray(L0_attn_Wi).T, KX),
        "wgT": chunked(np.asarray(L0_attn_Wg).T, KH),
        "woT": chunked(np.asarray(L0_attn_Wo).T, KH),
        "w1T": chunked(np.asarray(L0_ffn_w1).T, KX),
        "w2T": chunked(np.asarray(L0_ffn_w2).T, KF),
        "params": np.ascontiguousarray(np.concatenate(
            [conv_w, cols(L0_attn_conv_b), cols(L0_attn_bg), cols(L0_attn_forget_base), cols(L0_ffn_b1)], axis=1)),
        "rows": np.ascontiguousarray(np.stack([np.asarray(L0_tok_b), np.asarray(L0_ffn_b2)])),
    }
    nc = bacc.Bacc("TRN2", target_bir_lowering=False, num_devices=1)
    args = [nc.dram_tensor(name, a.shape, F32, kind="ExternalInput").ap() for name, a in arrays.items()]
    out = nc.dram_tensor("out", (NSEQ, T, DIM), F32, kind="ExternalOutput").ap()
    tower(nc, *args, out.rearrange("s (t p) d -> s p t d", p=TT))
    r = run_bass_kernel_spmd(nc, [arrays], core_ids=[0])
    return r.results[0]["out"]
```

```python
from contextlib import ExitStack

import concourse.bass as bass
from concourse import mybir

ALU = mybir.AluOpType
ACT = mybir.ActivationFunctionType
F32 = mybir.dt.float32
F32R = mybir.dt.float32r

P = 128
NSEQ = 16
T_IN = 375
DIM = 256
SHIFTS = (0, 3, 6)
T = T_IN - SHIFTS[-1]
TP = T + 1
TT = 123
NT = T // TT
KX = DIM // P
HID = 384
KH = HID // P
FF = 1024
KF = FF // P
PART = ((0, 5), (5, 8))
LAST_PART = ((0, 3), (3, 6), (6, 8))
TAPS = 4
NJ = len(SHIFTS) * KX
LN_EPS = 1e-5
BETA_EPS = 1e-6
GATE_C = -8.0
S_CONVW, S_CONVB, S_BG, S_BASE, S_B1 = 0, 12, 15, 21, 24
S_COLS = 32
SP_STEPS = 20

BANK_FG = (7, 0, 1, 5, 6, 4)
BANK_T2 = (2, 3)
BANK_TOK = (7, 0, 1)
BANK_E = (5, 6, 4, 2, 3, 1, 5, 6)
BANK_T1 = (7, 0)
BANK_T1_FIRST = (5, 6)
BANK_E_NEXT_LAST = (7, 0, 1, 2, 3, 5, 6, 4)
BANK_ATT_LAST = (7, 0, 1)
BANK_T2_LAST = (7, 0)
BANK_FFN_LAST = (7, 0, 4)
BANK_U = (7, 0, 1)
BANK_GATE = (2, 3, 4)
BANK_ATT = (5, 6, 4)
BANK_FFN = 2


def need(eng, sem, value):
    if isinstance(value, int) and value <= 0:
        return
    eng.wait_ge(sem, value)


def parts(n):
    return LAST_PART if at(n, NSEQ - 1) else PART


def e_banks(n):
    return BANK_E_NEXT_LAST if at(n, NSEQ - 2) else BANK_E


def at(i, k):
    return isinstance(i, int) and i == k


def tower(nc, xT, wtokT, wiT, wgT, woT, w1T, w2T, params, rows, out):
    with ExitStack() as ctx:
        def sb(name, shape, dt=F32):
            return ctx.enter_context(nc.sbuf_tensor(name, shape, dt))

        def sem(name):
            return ctx.enter_context(nc.semaphore(name))

        ps = ctx.enter_context(nc.psum_tensor("ps", [P, 8, 512], F32))

        tok_wh, tok_wl = sb("tok_wh", [P, NJ, DIM], F32R), sb("tok_wl", [P, NJ, DIM], F32R)
        wi_h, wi_l = sb("wi_h", [P, KX, 2 * HID], F32R), sb("wi_l", [P, KX, 2 * HID], F32R)
        wg_h, wg_l = sb("wg_h", [P, KH, 2 * HID], F32R), sb("wg_l", [P, KH, 2 * HID], F32R)
        wo_h, wo_l = sb("wo_h", [P, KH, DIM], F32R), sb("wo_l", [P, KH, DIM], F32R)
        w1_sign = sb("w1_sign", [P, KX, FF], F32R)
        w2_sign = sb("w2_sign", [P, KF, DIM], F32R)
        stage_a, stage_b = sb("stage_a", [P, 2048]), sb("stage_b", [P, 2048])
        par = sb("par", [P, S_COLS])
        row = sb("row", [P, 2, DIM])
        alpha1 = sb("alpha1", [P, KF])
        alpha2 = sb("alpha2", [P, DIM])
        half_bg = sb("half_bg", [P, 2 * KH])
        decay_c = sb("decay_c", [P, KH])
        sp = sb("sp", [P, 6, KH])
        ident = sb("ident", [P, P])
        ones = sb("ones", [P, P])
        mhalf = sb("mhalf", [P, NT])
        ln_bias = sb("ln_bias", [P, 1])

        tok_raw = stage_a[:, 0:NJ * DIM].rearrange("p (j o) -> p j o", j=NJ)

        x_raw = sb("x_raw", [P, 2, KX, T_IN])
        x_h, x_l = sb("x_h", [P, KX, T_IN], F32R), sb("x_l", [P, KX, T_IN], F32R)
        h = sb("h", [P, 2, NT, DIM])
        outb = sb("outb", [P, 2, NT, DIM])
        ffn_s = sb("ffn_s", [P, NT, DIM])
        xn1, xn2 = sb("xn1", [P, NT, DIM]), sb("xn2", [P, NT, DIM])
        stats = [sb(f"stats{j}", [P, NT, 6]) for j in (0, 1)]
        moment = [sb(f"moment{j}", [P, NT, 5]) for j in (0, 1)]
        mean = [sb(f"mean{j}", [P, NT]) for j in (0, 1)]
        var_eps = [sb(f"var_eps{j}", [P, NT]) for j in (0, 1)]
        rstd = [sb(f"rstd{j}", [P, NT]) for j in (0, 1)]
        xa_h, xa_l = sb("xa_h", [P, KX, TP], F32R), sb("xa_l", [P, KX, TP], F32R)
        xb_h, xb_l = sb("xb_h", [P, KX, TP], F32R), sb("xb_l", [P, KX, TP], F32R)
        uc = sb("uc", [P, KH, T])
        u_h, u_l = sb("u_h", [P, KH, TP], F32R), sb("u_l", [P, KH, TP], F32R)
        x1_h, x1_l = (u[:, :, :].rearrange("p a b -> p (a b)")[:, 0:KX * T_IN].rearrange("p (a b) -> p a b", a=KX)
                      for u in (u_h, u_l))
        gate = sb("gate", [P, 2, KH, T])
        decay = sb("decay", [P, KH, T])
        beta = sb("beta", [P, KH, T])
        state = sb("state", [P, KH, T])
        y_h, y_l = sb("y_h", [P, KH, T], F32R), sb("y_l", [P, KH, T], F32R)
        g = sb("g", [P, KF, T])
        stage_c = g[:, :, :].rearrange("p a b -> p (a b)")[:, 0:KH * 2 * HID]
        g_h, g_l = sb("g_h", [P, KF, T], F32R), sb("g_l", [P, KF, T], F32R)

        in_x = [sem("in_x0"), sem("in_x1")]
        in_tok = [sem("in_tok0"), sem("in_tok1")]
        in_wi, in_wg, in_wo = sem("in_wi"), sem("in_wg"), sem("in_wo")
        in_w1, in_w2, in_par, in_row = sem("in_w1"), sem("in_w2"), sem("in_par"), sem("in_row")
        out_stored = [sem("out_stored0"), sem("out_stored1")]
        consts_ready, ident_zero, ident_ready, pads_ready = (
            sem("consts_ready"), sem("ident_zero"), sem("ident_ready"), sem("pads_ready"))
        w_hi, w_lo = sem("w_hi"), sem("w_lo")
        sp_step, sp_exp = sem("sp_step"), sem("sp_exp")
        sign_part, signs_ready = sem("sign_part"), sem("signs_ready")
        folded = sem("folded")
        abs_ready, alpha_sum, alpha_ready = sem("abs_ready"), sem("alpha_sum"), sem("alpha_ready")
        x_hi, x_split = sem("x_hi"), sem("x_split")
        tok_done, h_ready = sem("tok_done"), sem("h_ready")
        bn_ready = [sem("bn_ready1"), sem("bn_ready2")]
        sums_ready, terms_ready = [sem("sums1"), sem("sums2")], [sem("terms1"), sem("terms2")]
        veps_ready, rstd_ready = [sem("veps1"), sem("veps2")], [sem("rstd1"), sem("rstd2")]
        xn1_ready, t1_done, xa_hi, xa_lo = sem("xn1_ready"), sem("t1_done"), sem("xa_hi"), sem("xa_lo")
        gi_done = sem("gi_done")
        tap0_ready, taps, u_hi, u_lo = sem("tap0_ready"), sem("taps"), sem("u_hi"), sem("u_lo")
        gate_ready = sem("gate_ready")
        fg_done, tanh_ready = sem("fg_done"), sem("tanh_ready")
        decay_ready, sq_ready, ln_ready, beta_ready = (
            sem("decay_ready"), sem("sq_ready"), sem("ln_ready"), sem("beta_ready"))
        v_ready, xt_ready, scanned, y_ready, y_hi, y_lo = (
            sem("v_ready"), sem("xt_ready"), sem("scanned"), sem("y_ready"), sem("y_hi"), sem("y_lo"))
        att_done, h2_ready = sem("att_done"), sem("h2_ready")
        xn2_ready, t2_done, xb_hi, xb_lo = sem("xn2_ready"), sem("t2_done"), sem("xb_hi"), sem("xb_lo")
        ff1_done, g_ready, g_hi, g_lo = sem("ff1_done"), sem("g_ready"), sem("g_hi"), sem("g_lo")
        ffn_done, ffn_scaled, outb_ready, out_ready = (
            sem("ffn_done"), sem("ffn_scaled"), sem("outb_ready"), sem("out_ready"))

        def raw(a):
            return a.bitcast(F32)

        def steps(eng, body):
            for i in (0, 1):
                body(i, i % 2)
            with eng.Fori(1, NSEQ // 2 - 1) as pair:
                body(2 * pair, 0)
                body(2 * pair + 1, 1)
            for i in (NSEQ - 2, NSEQ - 1):
                body(i, i % 2)

        def exists(i):
            return not isinstance(i, int) or 0 <= i < NSEQ

        block = ctx.enter_context(nc.Block())

        @block.sync
        def _(sp_eng):
            def load(n, p):
                need(sp_eng, x_split, n - 1)
                sp_eng.dma_start(x_raw[:, p], xT[n]).then_inc(in_x[p], 16)

            def store(n, p):
                need(sp_eng, out_ready, n + 1)
                sp_eng.dma_start(out[n], outb[0:TT, p]).then_inc(out_stored[p], 16)

            def store_tiles(n, p):
                for t in range(NT):
                    sp_eng.wait_ge(out_ready, n + 1 + t)
                    sp_eng.dma_start(out[n][:, t], outb[0:TT, p, t]).then_inc(out_stored[p], 16)

            load(0, 0)
            for k in (0, 1):
                cols = slice(k * NJ // 2 * DIM, (k + 1) * NJ // 2 * DIM)
                sp_eng.dma_start(stage_a[:, cols], wtokT[:, cols]).then_inc(in_tok[k], 16)
            sp_eng.dma_start(stage_b[:, 0:KX * 2 * HID], wiT).then_inc(in_wi, 16)
            load(1, 1)
            sp_eng.dma_start(stage_c[:, :], wgT).then_inc(in_wg, 16)
            sp_eng.wait_ge(w_hi, 2)
            sp_eng.wait_ge(w_lo, 2)
            sp_eng.dma_start(stage_a[:, :], w1T).then_inc(in_w1, 16)
            sp_eng.wait_ge(w_hi, 4)
            sp_eng.wait_ge(w_lo, 3 + KH)
            sp_eng.dma_start(stage_c[:, 0:KH * DIM], woT).then_inc(in_wo, 16)
            sp_eng.dma_start(stage_b[:, :], w2T).then_inc(in_w2, 16)

            def body(i, p):
                if exists(i + 2):
                    load(i + 2, p)
                if exists(i - 1):
                    store(i - 1, 1 - p)

            steps(sp_eng, body)
            store_tiles(NSEQ - 1, (NSEQ - 1) % 2)
            sp_eng.wait_ge(out_stored[0], 16 * (NSEQ // 2))
            sp_eng.wait_ge(out_stored[1], 16 * (NSEQ // 2 - 1 + NT))

        @block.gpsimd
        def _(pool):
            pool.memset(ident[:, :], 0.0).then_inc(ident_zero, 1)
            pool.memset(ones[:, :], 1.0).then_inc(consts_ready, 1)
            pool.memset(mhalf[:, :], -0.5).then_inc(consts_ready, 1)
            pool.memset(ln_bias[:, :], 0.25 * (1.0 + BETA_EPS)).then_inc(consts_ready, 1)
            for padded in (xa_h, xa_l, xb_h, xb_l):
                pool.memset(raw(padded[:, :, T:TP]), 0.0).then_inc(pads_ready, 1)
            pool.wait_ge(ident_zero, 1)
            pool.affine_select(out=ident[:, :], in_=ident[:, :], compare_op=ALU.not_equal, fill=1.0, base=0,
                               pattern=[[-1, P]], channel_multiplier=1).then_inc(ident_ready, 1)
            pool.wait_ge(consts_ready, 3)

            def split_x(n, p):
                pool.wait_ge(x_hi, n + 1)
                hi, lo = (x1_h, x1_l) if at(n, 1) else (x_h[:, :, :], x_l[:, :, :])
                pool.tensor_tensor(lo, x_raw[:, p], raw(hi), ALU.subtract).then_inc(x_split, 1)

            def rsqrt(n, which):
                pool.wait_ge(veps_ready[which], n + 1)
                pool.tensor_tensor(rstd[which][0:TT, :], var_eps[which][0:TT, :], mhalf[0:TT, :],
                                   ALU.pow).then_inc(rstd_ready[which], 1)

            def residual(n, p):
                rsqrt(n, 1)
                if not at(n, 0) and not at(n, 1):
                    pool.wait_ge(out_stored[p], 8 * (n - p))
                for t in range(NT):
                    ins = pool.tensor_tensor(outb[0:TT, p, t], h[0:TT, p, t], row[0:TT, 1], ALU.add)
                ins.then_inc(outb_ready, 1)

            folds = []

            def fold(k, stage, columns):
                pool.wait_ge(abs_ready, k + 1)
                half = KX * FF // 2
                while half >= columns:
                    pool.tensor_tensor(stage[:, 0:half], stage[:, 0:half], stage[:, half:2 * half],
                                       ALU.add).then_inc(folded, 1)
                    folds.append(half)
                    if half > columns:
                        pool.wait_ge(folded, len(folds))
                    half //= 2

            def body(i, p):
                if at(i, 1):
                    residual(0, 0)
                if exists(i + 1) and not at(i, 0):
                    rsqrt(i + 1, 0)
                if at(i, 1):
                    fold(1, stage_b, DIM)
                if exists(i + 2):
                    split_x(i + 2, p)
                if at(i, 0):
                    fold(0, stage_a, FF)
                else:
                    residual(i, p)
                if exists(i - 1):
                    finish(i - 1, 1 - p)

            def finish(n, p):
                pool.wait_ge(outb_ready, n + 1)
                pool.wait_ge(ffn_scaled, n + 1)
                pool.tensor_tensor(outb[0:TT, p], outb[0:TT, p], ffn_s[0:TT], ALU.add).then_inc(out_ready, 1)

            split_x(0, 0)
            split_x(1, 1)
            rsqrt(0, 0)
            rsqrt(1, 0)
            pool.wait_ge(tok_done, 6)
            for padded in (u_h, u_l):
                pool.memset(raw(padded[:, :, T:TP]), 0.0).then_inc(pads_ready, 1)
            pool.wait_ge(in_row, 16)
            steps(pool, body)

        @block.scalar
        def _(act):
            act.dma_start(par[:, :], params).then_inc(in_par, 16)
            act.dma_start(row[:, :, :], rows.partition_broadcast(P)).then_inc(in_row, 16)

            act.wait_ge(sp_step, 2)
            act.activation(sp[:, 2], sp[:, 1], ACT.Exp, scale=-1.0).then_inc(sp_exp, 1)

            def hi_part(dst, src, arrived):
                act.wait_ge(arrived, 16)
                act.activation(dst, src, ACT.Copy).then_inc(w_hi, 1)

            def magnitudes(k, stage):
                act.wait_ge(signs_ready, k + 1)
                act.activation(stage[:, :], stage[:, :], ACT.Abs).then_inc(abs_ready, 1)

            def x_part(n, p):
                act.wait_ge(in_x[p], 8 * (n - p) + 16)
                if not at(n, 1):
                    need(act, tok_done, 3 * n)
                dst = x1_h if at(n, 1) else x_h[:, :, :]
                act.activation(dst, x_raw[:, p], ACT.Copy).then_inc(x_hi, 1)

            x_part(0, 0)
            for k in (0, 1):
                js = slice(k * NJ // 2, (k + 1) * NJ // 2)
                hi_part(tok_wh[:, js], tok_raw[:, js], in_tok[k])
            x_part(1, 1)
            hi_part(wi_h[:, :, :].rearrange("p a b -> p (a b)"), stage_b[:, 0:KX * 2 * HID], in_wi)
            hi_part(wg_h[:, :, :].rearrange("p a b -> p (a b)"), stage_c[:, :], in_wg)

            def xa_parts(n, banks):
                for c in range(KX):
                    act.wait_ge(t1_done, 2 * n + c + 1)
                    if c == 0:
                        need(act, gi_done, 6 * n)
                    act.activation(xa_h[:, c, 0:T], ps[:, banks[c], 0:T], ACT.Copy).then_inc(xa_hi, 1)

            def last_tap(n, chunks=range(KH)):
                for c in chunks:
                    act.wait_ge(gi_done, 6 * n + c + 1)
                    if c == 0:
                        need(act, v_ready, n)
                        need(act, u_lo, 3 * n)
                    act.activation(uc[:, c], ps[:, BANK_U[c], 0:T], ACT.Identity,
                                   scale=par[:, S_CONVW + TAPS * c + 3:S_CONVW + TAPS * c + 4],
                                   bias=par[:, S_CONVB + c:S_CONVB + c + 1]).then_inc(tap0_ready, 1)

            def gate_gelu(n, p):
                for c in range(KH):
                    act.wait_ge(gi_done, 6 * n + KH + c + 1)
                    if c == 0:
                        need(act, y_ready, n - 1)
                    act.activation(gate[:, p, c], ps[:, BANK_GATE[c], 0:T], ACT.Gelu).then_inc(gate_ready, 1)

            def u_parts(n):
                need(act, fg_done, 6 * n)
                for c in range(KH):
                    act.wait_ge(taps, 9 * n + 6 + c + 1)
                    act.activation(u_h[:, c, 0:T], uc[:, c], ACT.Copy).then_inc(u_hi, 1)

            def gates_tanh(n, ms=range(2 * KH)):
                for m in ms:
                    act.wait_ge(fg_done, 6 * n + m + 1)
                    if m == 0:
                        need(act, scanned, 3 * n)
                    if m == KH:
                        need(act, y_lo, n)
                    dst = decay[:, m] if m < KH else state[:, m - KH]
                    act.activation(dst, ps[:, BANK_FG[m], 0:T], ACT.Tanh, scale=0.5,
                                   bias=half_bg[:, m:m + 1]).then_inc(tanh_ready, 1)

            def xb_parts(n, banks=BANK_T2):
                for c in range(KX):
                    act.wait_ge(t2_done, 2 * n + c + 1)
                    if c == 0:
                        need(act, ff1_done, 8 * n)
                    act.activation(xb_h[:, c, 0:T], ps[:, banks[c], 0:T], ACT.Copy).then_inc(xb_hi, 1)

            def decays(n):
                act.preload_act_table_set("natural_log_exp_and_others")
                for c in range(KH):
                    if at(n, 0):
                        last_tap(1, [c])
                    act.wait_ge(tanh_ready, 6 * n + c + 1)
                    act.activation(decay[:, c], decay[:, c], ACT.Exp, scale=decay_c[:, c:c + 1],
                                   bias=decay_c[:, c:c + 1]).then_inc(decay_ready, 1)
                if at(n, NSEQ - 1):
                    xb_parts(n - 1)
                else:
                    act.wait_ge(decay_ready, 3 * n + 3)
                    need(act, xt_ready, n)
                    act.activation(beta[:, :, :], decay[:, :, :], ACT.Square).then_inc(sq_ready, 1)
                act.wait_ge(sq_ready, n + 1)
                act.activation(beta[:, :, :], beta[:, :, :], ACT.Ln, scale=-0.25,
                               bias=ln_bias[:, 0:1]).then_inc(ln_ready, 1)
                act.wait_ge(ln_ready, n + 1)
                act.activation(beta[:, :, :], beta[:, :, :], ACT.Exp, scale=0.5).then_inc(beta_ready, 1)

            def ffn_gelu(n, half, chunks=None):
                for c in chunks or range(*parts(n)[half]):
                    act.wait_ge(ff1_done, 8 * n + c + 1)
                    if c == parts(n)[half][0]:
                        need(act, g_lo, 2 * n if at(n, NSEQ - 1) else 2 * n - 1 + half)
                    act.activation(g[:, c], ps[:, e_banks(n)[c], 0:T], ACT.Gelu, scale=alpha1[:, c:c + 1],
                                   bias=par[:, S_B1 + c:S_B1 + c + 1]).then_inc(g_ready, 1)

            def ffn_hi(n, half):
                a, b = parts(n)[half]
                act.wait_ge(g_ready, 8 * n + b)
                need(act, ffn_done, n)
                act.activation(g_h[:, a:b], g[:, a:b],
                               ACT.Copy).then_inc(g_hi, 1)

            def y_part_chunk(n, c):
                act.wait_ge(y_ready, n + 1 + c)
                if c == 0:
                    act.wait_ge(att_done, 3 * n)
                act.activation(y_h[:, c], state[:, c], ACT.Copy).then_inc(y_hi, 1)

            def y_part(n):
                act.wait_ge(y_ready, n + 1)
                need(act, att_done, 3 * n)
                act.activation(y_h[:, :, :], state[:, :, :], ACT.Copy).then_inc(y_hi, 1)

            act.wait_ge(in_par, 16)
            xa_parts(0, BANK_T1_FIRST)
            last_tap(0)
            gate_gelu(0, 0)
            xa_parts(1, BANK_T1_FIRST)
            u_parts(0)
            hi_part(wo_h[:, :, :].rearrange("p a b -> p (a b)"), stage_c[:, 0:KH * DIM], in_wo)

            def first(i, p):
                gates_tanh(0)
                act.wait_ge(sp_step, SP_STEPS)
                decays(0)
                u_parts(1)
                gate_gelu(1, 1)
                y_part(0)
                x_part(2, 0)
                magnitudes(0, stage_a)

            def last(i, p):
                n = NSEQ - 1
                gates_tanh(n, range(KH))
                decays(n)
                gates_tanh(n, range(KH, 2 * KH))
                ffn_gelu(n - 1, 0, range(0, 3))
                y_part_chunk(n, 0)
                ffn_gelu(n - 1, 0, range(3, 4))
                y_part_chunk(n, 1)
                ffn_gelu(n - 1, 0, range(4, 5))
                y_part_chunk(n, 2)
                ffn_hi(n - 1, 0)
                ffn_gelu(n - 1, 1)
                ffn_hi(n - 1, 1)

            def body(i, p):
                if at(i, 0):
                    return first(i, p)
                if at(i, NSEQ - 1):
                    return last(i, p)
                gates_tanh(i)
                if at(i, 1):
                    magnitudes(1, stage_b)
                    decays(i)
                    xb_parts(i - 1)
                    act.wait_ge(w_lo, 4 + KH)
                    act.wait_ge(alpha_ready, 1)
                else:
                    xb_parts(i - 1)
                    decays(i)
                ffn_gelu(i - 1, 0, range(0, 4))
                xa_parts(i + 1, BANK_T1)
                ffn_gelu(i - 1, 0, range(4, 5))
                ffn_hi(i - 1, 0)
                ffn_gelu(i - 1, 1)
                y_part(i)
                last_tap(i + 1)
                ffn_hi(i - 1, 1)
                gate_gelu(i + 1, 1 - p)
                if exists(i + 2):
                    x_part(i + 2, p)
                u_parts(i + 1)

            steps(act, body)
            n = NSEQ - 1
            xb_parts(n, BANK_T2_LAST)
            for part in range(len(parts(n))):
                ffn_gelu(n, part)
                ffn_hi(n, part)

        @block.vector
        def _(dve):
            step = [0]

            def sp_op(ins):
                step[0] += 1
                ins.then_inc(sp_step, 1)
                dve.wait_ge(sp_step, step[0])

            dve.wait_ge(in_par, 16)
            base = par[:, S_BASE:S_BASE + KH]
            sp_op(dve.tensor_scalar(sp[:, 0], base, -1.0, None, ALU.mult))
            sp_op(dve.tensor_tensor(sp[:, 1], base, sp[:, 0], ALU.max))
            sp_op(dve.tensor_scalar(half_bg[:, :], par[:, S_BG:S_BG + 2 * KH], 0.5, None, ALU.mult))

            def softplus():
                dve.wait_ge(sp_exp, 1)
                sp_op(dve.tensor_scalar(sp[:, 3], sp[:, 2], 2.0, None, ALU.add))
                sp_op(dve.reciprocal(sp[:, 4], sp[:, 3]))
                sp_op(dve.tensor_tensor(sp[:, 2], sp[:, 2], sp[:, 4], ALU.mult))
                sp_op(dve.tensor_tensor(sp[:, 3], sp[:, 2], sp[:, 2], ALU.mult))
                last = 9
                for k in range(last, 0, -1):
                    src = sp[:, 4] if k < last else sp[:, 5]
                    if k == last:
                        ins = dve.memset(sp[:, 5], 0.0)
                        ins.then_inc(sp_step, 1)
                        step[0] += 1
                        dve.wait_ge(sp_step, step[0])
                    sp_op(dve.scalar_tensor_tensor(out=sp[:, 4], in0=src, scalar=1.0 / (2 * k + 1), in1=sp[:, 3],
                                                   op0=ALU.add, op1=ALU.mult))
                sp_op(dve.scalar_tensor_tensor(out=sp[:, 4], in0=sp[:, 4], scalar=1.0, in1=sp[:, 2],
                                               op0=ALU.add, op1=ALU.mult))
                sp_op(dve.tensor_scalar(sp[:, 0], base, 0.0, 0.5 * GATE_C, ALU.max, ALU.mult))
                sp_op(dve.scalar_tensor_tensor(out=decay_c[:, :], in0=sp[:, 4], scalar=GATE_C, in1=sp[:, 0],
                                               op0=ALU.mult, op1=ALU.add))
                assert step[0] == SP_STEPS

            def lo_part(k, dst, src, hi):
                dve.wait_ge(w_hi, k)
                dve.tensor_tensor(dst, src, raw(hi), ALU.subtract).then_inc(w_lo, 1)

            def flat(a):
                return a[:, :, :].rearrange("p a b -> p (a b)")

            for k in (0, 1):
                js = slice(k * NJ // 2, (k + 1) * NJ // 2)
                lo_part(k + 1, tok_wl[:, js], tok_raw[:, js], tok_wh[:, js])
            lo_part(3, flat(wi_l), stage_b[:, 0:KX * 2 * HID], flat(wi_h))

            def signs(k, dst, stage, arrived):
                dve.wait_ge(arrived, 16)
                dve.tensor_scalar(dst, stage, 0.0, None, ALU.is_lt).then_inc(sign_part, 1)
                dve.wait_ge(sign_part, k)
                dve.scalar_tensor_tensor(out=dst, in0=stage, scalar=0.0, in1=raw(dst), op0=ALU.is_gt,
                                         op1=ALU.subtract).then_inc(signs_ready, 1)

            def add_tok(n, p):
                for t in range(NT):
                    dve.wait_ge(tok_done, 3 * n + t + 1)
                    if t == 0:
                        need(dve, outb_ready, n - 1)
                    dve.tensor_tensor(h[0:TT, p, t], ps[0:TT, BANK_TOK[t], 0:DIM], row[0:TT, 0],
                                      ALU.add).then_inc(h_ready, 1)
                    dve.wait_ge(h_ready, 3 * n + t + 1)
                    dve.bn_stats(stats[0][0:TT, t], h[0:TT, p, t]).then_inc(bn_ready[0], 1)

            def moments(n, which):
                st, mo = stats[which][0:TT], moment[which]
                dve.wait_ge(bn_ready[which], 3 * n + 3)
                dve.tensor_tensor(mo[0:TT, :, 0:2], st[:, :, 1:3], st[:, :, 4:6], ALU.add).then_inc(sums_ready[which], 1)
                dve.tensor_tensor(mo[0:TT, :, 2], st[:, :, 1], st[:, :, 4], ALU.subtract).then_inc(sums_ready[which], 1)
                dve.wait_ge(sums_ready[which], 2 * n + 2)
                dve.tensor_scalar(mo[0:TT, :, 3], mo[0:TT, :, 1], 1.0 / DIM, LN_EPS, ALU.mult,
                                  ALU.add).then_inc(terms_ready[which], 1)
                dve.scalar_tensor_tensor(out=mo[0:TT, :, 4], in0=mo[0:TT, :, 2], scalar=0.25, in1=mo[0:TT, :, 2],
                                         op0=ALU.mult, op1=ALU.mult).then_inc(terms_ready[which], 1)
                dve.tensor_scalar(mean[which][0:TT, :], mo[0:TT, :, 0], 0.5, None, ALU.mult).then_inc(
                    terms_ready[which], 1)
                dve.wait_ge(terms_ready[which], 3 * n + 3)
                dve.tensor_tensor(var_eps[which][0:TT, :], mo[0:TT, :, 3], mo[0:TT, :, 4], ALU.add).then_inc(
                    veps_ready[which], 1)

            def norm(n, p, which, xn, ready, transposed):
                dve.wait_ge(rstd_ready[which], n + 1)
                need(dve, transposed, 2 * n)
                for t in range(NT):
                    dve.tensor_scalar(xn[0:TT, t], h[0:TT, p, t], mean[which][0:TT, t:t + 1],
                                      rstd[which][0:TT, t:t + 1], ALU.subtract, ALU.mult).then_inc(ready, 1)

            def xa_low(n, banks):
                for c in range(KX):
                    dve.wait_ge(xa_hi, 2 * n + c + 1)
                    dve.tensor_tensor(xa_l[:, c, 0:T], ps[:, banks[c], 0:T], raw(xa_h[:, c, 0:T]),
                                      ALU.subtract).then_inc(xa_lo, 1)

            def conv(n, delays):
                for d in delays:
                    for c in range(KH):
                        if d == 1:
                            dve.wait_ge(tap0_ready, 3 * n + c + 1)
                        else:
                            dve.wait_ge(taps, 9 * n + 3 * (d - 2) + c + 1)
                        w = S_CONVW + TAPS * c + 3 - d
                        dve.scalar_tensor_tensor(out=uc[:, c, d:T], in0=ps[:, BANK_U[c], 0:T - d],
                                                 scalar=par[:, w:w + 1], in1=uc[:, c, d:T],
                                                 op0=ALU.mult, op1=ALU.add).then_inc(taps, 1)

            def u_low(n):
                for c in range(KH):
                    dve.wait_ge(u_hi, 3 * n + c + 1)
                    dve.tensor_tensor(u_l[:, c, 0:T], uc[:, c], raw(u_h[:, c, 0:T]), ALU.subtract).then_inc(u_lo, 1)

            def input_term(n):
                dve.wait_ge(tanh_ready, 6 * n + 6)
                dve.scalar_tensor_tensor(out=state[:, :, :], in0=state[:, :, :], scalar=1.0, in1=uc[:, :, :],
                                         op0=ALU.add, op1=ALU.mult).then_inc(v_ready, 1)

            def xb_low(n, banks=BANK_T2):
                for c in range(KX):
                    dve.wait_ge(xb_hi, 2 * n + c + 1)
                    dve.tensor_tensor(xb_l[:, c, 0:T], ps[:, banks[c], 0:T], raw(xb_h[:, c, 0:T]),
                                      ALU.subtract).then_inc(xb_lo, 1)

            def scale_input(n):
                dve.wait_ge(v_ready, n + 1)
                dve.wait_ge(beta_ready, n + 1)
                dve.tensor_tensor(state[:, :, :], state[:, :, :], beta[:, :, :], ALU.mult).then_inc(xt_ready, 1)

            def recur(n):
                dve.wait_ge(xt_ready, n + 1)
                for c in range(KH):
                    dve.tensor_tensor_scan(state[:, c], decay[:, c], state[:, c], 0.0, ALU.mult,
                                           ALU.add).then_inc(scanned, 1)

            def gated(n, p):
                dve.wait_ge(scanned, 3 * n + 3)
                dve.wait_ge(gate_ready, 3 * n + 3)
                dve.tensor_tensor(state[:, :, :], state[:, :, :], gate[:, p], ALU.mult).then_inc(y_ready, 1)

            def y_low(n):
                dve.wait_ge(y_hi, n + 1)
                dve.tensor_tensor(y_l[:, :, :], state[:, :, :], raw(y_h[:, :, :]), ALU.subtract).then_inc(y_lo, 1)

            def ffn_low(n, half):
                a, b = parts(n)[half]
                dve.wait_ge(g_hi, 2 * n + half + 1)
                dve.tensor_tensor(g_l[:, a:b], g[:, a:b], raw(g_h[:, a:b]), ALU.subtract).then_inc(g_lo, 1)

            def add_att(n, p):
                banks = BANK_ATT_LAST if at(n, NSEQ - 1) else BANK_ATT
                for t in range(NT):
                    dve.wait_ge(att_done, 3 * n + t + 1)
                    dve.tensor_tensor(h[0:TT, p, t], h[0:TT, p, t], ps[0:TT, banks[t], 0:DIM],
                                      ALU.add).then_inc(h2_ready, 1)
                for t in range(NT):
                    dve.wait_ge(h2_ready, 3 * n + t + 1)
                    dve.bn_stats(stats[1][0:TT, t], h[0:TT, p, t]).then_inc(bn_ready[1], 1)
                moments(n, 1)

            def scale_ffn(n):
                dve.wait_ge(ffn_done, n + 1)
                need(dve, out_ready, n)
                prod = ps[0:TT, BANK_FFN:BANK_FFN + 2].rearrange("p b n -> p (b n)")
                for t in range(NT):
                    ins = dve.tensor_tensor(ffn_s[0:TT, t], prod[:, t * DIM:(t + 1) * DIM], alpha2[0:TT, :],
                                            ALU.mult)
                ins.then_inc(ffn_scaled, 1)

            def wg_low(k):
                cols = slice(k * 2 * HID, (k + 1) * 2 * HID)
                lo_part(4, wg_l[:, k], stage_c[:, cols], wg_h[:, k])

            dve.wait_ge(in_row, 16)
            add_tok(0, 0)
            moments(0, 0)
            norm(0, 0, 0, xn1, xn1_ready, t1_done)
            add_tok(1, 1)
            wg_low(0)
            xa_low(0, BANK_T1_FIRST)
            moments(1, 0)
            wg_low(1)
            norm(1, 1, 0, xn1, xn1_ready, t1_done)
            wg_low(2)
            conv(0, (1, 2, 3))
            u_low(0)
            xa_low(1, BANK_T1_FIRST)
            softplus()
            lo_part(5, flat(wo_l), stage_c[:, 0:KH * DIM], flat(wo_h))

            def first(i, p):
                signs(1, flat(w1_sign), stage_a[:, :], in_w1)
                input_term(0)
                conv(1, (1, 2, 3))
                scale_input(0)
                u_low(1)
                recur(0)
                gated(0, 0)
                y_low(0)
                signs(2, flat(w2_sign), stage_b[:, :], in_w2)

            def last(i, p):
                n = NSEQ - 1
                for c in range(KH):
                    dve.wait_ge(decay_ready, 3 * n + c + 1)
                    ins = dve.tensor_tensor(beta[:, c], decay[:, c], decay[:, c], ALU.mult)
                ins.then_inc(sq_ready, 1)
                xb_low(n - 1)

                def input_chunk(c):
                    dve.wait_ge(tanh_ready, 6 * n + KH + c + 1)
                    dve.scalar_tensor_tensor(out=state[:, c], in0=state[:, c], scalar=1.0, in1=uc[:, c],
                                             op0=ALU.add, op1=ALU.mult).then_inc(v_ready, 1)

                def scale_chunk(c):
                    if c == 0:
                        dve.wait_ge(beta_ready, n + 1)
                    dve.wait_ge(v_ready, n + 1 + c)
                    dve.tensor_tensor(state[:, c], state[:, c], beta[:, c], ALU.mult).then_inc(xt_ready, 1)

                def scan_chunk(c):
                    dve.wait_ge(xt_ready, n + 1 + c)
                    dve.tensor_tensor_scan(state[:, c], decay[:, c], state[:, c], 0.0, ALU.mult,
                                           ALU.add).then_inc(scanned, 1)

                def gated_chunk(c):
                    dve.wait_ge(scanned, 3 * n + 1 + c)
                    if c == 0:
                        dve.wait_ge(gate_ready, 3 * n + 3)
                    dve.tensor_tensor(state[:, c], state[:, c], gate[:, p, c], ALU.mult).then_inc(y_ready, 1)

                def low_chunk(c):
                    dve.wait_ge(y_hi, n + 1 + c)
                    dve.tensor_tensor(y_l[:, c], state[:, c], raw(y_h[:, c]), ALU.subtract).then_inc(y_lo, 1)

                input_chunk(0)
                input_chunk(1)
                scale_chunk(0)
                scale_chunk(1)
                scan_chunk(0)
                input_chunk(2)
                gated_chunk(0)
                scan_chunk(1)
                scale_chunk(2)
                gated_chunk(1)
                scan_chunk(2)
                low_chunk(0)
                gated_chunk(2)
                low_chunk(1)
                low_chunk(2)
                ffn_low(n - 1, 0)
                ffn_low(n - 1, 1)
                add_att(n, p)
                norm(n, p, 1, xn2, xn2_ready, t2_done)
                scale_ffn(n - 1)

            def body(i, p):
                if at(i, 0):
                    return first(i, p)
                if at(i, NSEQ - 1):
                    return last(i, p)
                input_term(i)
                if at(i, 1):
                    add_att(0, 0)
                    norm(0, 0, 1, xn2, xn2_ready, t2_done)
                    dve.wait_ge(alpha_sum, 1)
                    dve.tensor_scalar(alpha1[:, :], ps[:, BANK_ATT[2], 0:2 * KF:2], 1.0 / DIM, None,
                                      ALU.mult).then_inc(alpha_ready, 1)
                xb_low(i - 1)
                add_tok(i + 1, 1 - p)
                moments(i + 1, 0)
                scale_input(i)
                norm(i + 1, 1 - p, 0, xn1, xn1_ready, t1_done)
                recur(i)
                xa_low(i + 1, BANK_T1)
                gated(i, p)
                ffn_low(i - 1, 0)
                y_low(i)
                conv(i + 1, (1,))
                ffn_low(i - 1, 1)
                conv(i + 1, (2, 3))
                u_low(i + 1)
                if at(i, 1):
                    dve.wait_ge(alpha_sum, 2)
                    dve.tensor_scalar(alpha2[:, :], ps[:, BANK_FFN + 1, 0:DIM], 1.0 / FF, None,
                                      ALU.mult).then_inc(alpha_ready, 1)
                add_att(i, p)
                norm(i, p, 1, xn2, xn2_ready, t2_done)
                scale_ffn(i - 1)

            steps(dve, body)
            n = NSEQ - 1
            p = n % 2
            xb_low(n, BANK_T2_LAST)
            for part in range(len(parts(n))):
                ffn_low(n, part)
            dve.wait_ge(outb_ready, n + 1)
            dve.wait_ge(out_ready, n)
            for t in range(NT):
                dve.wait_ge(ffn_done, n + 1 + t)
                dve.tensor_tensor(ffn_s[0:TT, t], ps[0:TT, BANK_FFN_LAST[t], 0:DIM], alpha2[0:TT, :],
                                  ALU.mult).then_inc(ffn_scaled, 1)
                dve.wait_ge(ffn_scaled, n + 1 + t)
                dve.tensor_tensor(outb[0:TT, p, t], outb[0:TT, p, t], ffn_s[0:TT, t], ALU.add).then_inc(out_ready, 1)

        @block.tensor
        def _(pe):
            def split_product(acc, pairs, first=True, last=True):
                for k, (a, b) in enumerate(pairs):
                    ins = pe.matmul(acc, a, b, start=(first and k == 0), stop=(last and k == len(pairs) - 1))
                return ins

            def A(n):
                pe.wait_ge(x_split, n + 1)
                xs = (x1_h, x1_l) if at(n, 1) else (x_h, x_l)
                for t in range(NT):
                    if at(n, 1):
                        pe.wait_ge(h_ready, t + 1)
                    else:
                        need(pe, tanh_ready, 6 * (n - 1) + t + 1)
                    for j in range(NJ):
                        if at(n, 0) and t == 0 and j % (NJ // 2) == 0:
                            pe.wait_ge(w_lo, 1 + 2 * j // NJ)
                        f0 = t * TT + SHIFTS[j // KX]
                        xh, xl = (x[:, j % KX, f0:f0 + TT] for x in xs)
                        ins = split_product(ps[0:TT, BANK_TOK[t], 0:DIM],
                                            [(xh, tok_wh[:, j]), (xh, tok_wl[:, j]), (xl, tok_wh[:, j])],
                                            j == 0, j == NJ - 1)
                    ins.then_inc(tok_done, 1)

            def transposes(n, xn, ready, banks, done):
                for t in range(NT):
                    pe.wait_ge(ready, 3 * n + t + 1)
                    for c in range(KX):
                        ins = pe.transpose(ps[:, banks[c], t * TT:(t + 1) * TT], xn[0:TT, t, c * P:(c + 1) * P],
                                           ident[0:TT, 0:TT])
                        if t == NT - 1:
                            ins.then_inc(done, 1)

            def B(n, prev):
                for m in range(2 * KH):
                    held = {2: 5, 3: 3, 4: 4, 5: 2}
                    if exists(prev) and m in held:
                        pe.wait_ge(g_ready, 8 * prev + held[m] + 1)
                    if at(n, 0) and m < KH:
                        pe.wait_ge(h_ready, NT + m + 1)
                    if at(n, 1) and m in (0, 1, 2, 5):
                        pe.wait_ge(tanh_ready, m + 1)
                    bank = BANK_U[m] if m < KH else BANK_GATE[m - KH]
                    f0 = HID + m * P if m < KH else (m - KH) * P
                    for k in range(KX):
                        wh, wl = wi_h[:, k, f0:f0 + P], wi_l[:, k, f0:f0 + P]
                        if m == 0:
                            pe.wait_ge(xa_lo, 2 * n + k + 1)
                        ins = split_product(ps[:, bank, 0:TP], [(wh, xa_h[:, k]), (wl, xa_h[:, k]), (wh, xa_l[:, k])],
                                            k == 0, k == KX - 1)
                    ins.then_inc(gi_done, 1)

            def C(n, ms=range(2 * KH)):
                for m in ms:
                    if at(n, 1):
                        if m == 2 * KH - 1:
                            pe.wait_ge(gate_ready, 6)
                    elif m >= KH:
                        need(pe, h2_ready, 3 * (n - 1) + (m - KH) + 1)
                    if at(n, 0) and m == KH:
                        pe.wait_ge(xa_lo, 4)
                    for k in range(KH):
                        wh, wl = wg_h[:, k, m * P:(m + 1) * P], wg_l[:, k, m * P:(m + 1) * P]
                        if m == 0:
                            pe.wait_ge(u_lo, 3 * n + k + 1)
                        ins = split_product(ps[:, BANK_FG[m], 0:TP], [(wh, u_h[:, k]), (wl, u_h[:, k]), (wh, u_l[:, k])],
                                            k == 0, k == KH - 1)
                    ins.then_inc(fg_done, 1)

            def D(n, prev):
                banks = BANK_ATT_LAST if at(n, NSEQ - 1) else BANK_ATT
                for t in range(NT):
                    if at(n, 0):
                        pe.wait_ge(tanh_ready, 6 + KH + t + 1)
                    elif at(n, NSEQ - 1):
                        pe.wait_ge(g_ready, 8 * prev + t + 1)
                    elif t < 2:
                        pe.wait_ge(g_ready, 8 * prev + 7 + t)
                    else:
                        pe.wait_ge(gate_ready, 3 * (n + 1) + 3)
                    for k in range(KH):
                        if t == 0 and (k == 0 or at(n, NSEQ - 1)):
                            pe.wait_ge(y_lo, n + 1 + k)
                        yh, yl = (y[:, k, t * TT:(t + 1) * TT] for y in (y_h, y_l))
                        ins = split_product(ps[0:TT, banks[t], 0:DIM],
                                            [(yh, wo_h[:, k]), (yh, wo_l[:, k]), (yl, wo_h[:, k])],
                                            k == 0, k == KH - 1)
                    ins.then_inc(att_done, 1)

            def E(n, half):
                for c in range(*parts(n)[half]):
                    if at(n, 0) and c == 2:
                        pe.wait_ge(alpha_ready, 1)
                    if at(n, NSEQ - 2):
                        held = {0: 1, 1: 2, 2: 3, 5: 4, 6: 5, 7: 6}
                        if c in held:
                            pe.wait_ge(tanh_ready, 6 * (n + 1) + held[c])
                    elif c < 3 and exists(n + 1):
                        pe.wait_ge(tanh_ready, 6 * (n + 1) + 4 + c)
                    if at(n, NSEQ - 1) and c == 3:
                        pe.wait_ge(ffn_scaled, n)
                    if c >= 6 and not at(n, NSEQ - 2):
                        pe.wait_ge(g_ready, 8 * n + c - 5)
                    for k in range(KX):
                        if c == 0:
                            pe.wait_ge(xb_lo, 2 * n + k + 1)
                        w = w1_sign[:, k, c * P:(c + 1) * P]
                        ins = split_product(ps[:, e_banks(n)[c], 0:TP], [(w, xb_h[:, k]), (w, xb_l[:, k])],
                                            k == 0, k == KX - 1)
                    ins.then_inc(ff1_done, 1)

            def ffn_pairs(t, a, b):
                return [(gp[:, c, t * TT:(t + 1) * TT], w2_sign[:, c]) for c in range(a, b) for gp in (g_h, g_l)]

            def F(n):
                if exists(n + 2):
                    pe.wait_ge(gate_ready, 3 * (n + 2) + 2)
                if at(n, 0):
                    pe.wait_ge(alpha_ready, 2)
                prod = ps[0:TT, BANK_FFN:BANK_FFN + 2].rearrange("p b n -> p (b n)")
                for t in range(NT):
                    for k, (a, b) in enumerate(parts(n)):
                        if t == 0:
                            pe.wait_ge(g_lo, 2 * n + k + 1)
                        ins = split_product(prod[:, t * DIM:(t + 1) * DIM], ffn_pairs(t, a, b), a == 0, b == KF)
                ins.then_inc(ffn_done, 1)

            def F_last(n):
                for k, (a, b) in enumerate(parts(n)):
                    pe.wait_ge(g_lo, 2 * n + k + 1)
                    for t in range(NT):
                        ins = split_product(ps[0:TT, BANK_FFN_LAST[t], 0:DIM], ffn_pairs(t, a, b), a == 0, b == KF)
                        if b == KF:
                            ins.then_inc(ffn_done, 1)

            A(0)
            A(1)
            pe.wait_ge(ident_ready, 1)
            transposes(0, xn1, xn1_ready, BANK_T1_FIRST, t1_done)
            pe.wait_ge(w_lo, 3)
            pe.wait_ge(pads_ready, 4)
            B(0, -1)
            transposes(1, xn1, xn1_ready, BANK_T1_FIRST, t1_done)
            pe.wait_ge(w_lo, 3 + KH)
            pe.wait_ge(pads_ready, 6)

            def body(i, p):
                if at(i, 0):
                    C(0)
                    B(1, -1)
                    return
                if at(i, NSEQ - 1):
                    C(i, range(KH))
                    pe.wait_ge(ffn_scaled, i - 1)
                    transposes(i - 1, xn2, xn2_ready, BANK_T2, t2_done)
                    C(i, range(KH, 2 * KH))
                    E(i - 1, 0)
                    E(i - 1, 1)
                    D(i, i - 1)
                    F(i - 1)
                    return
                C(i)
                if at(i, 1):
                    pe.wait_ge(w_lo, 4 + KH)
                    D(0, -1)
                    A(2)
                    pe.wait_ge(consts_ready, 3)
                    pe.wait_ge(folded, 1)
                    pe.wait_ge(h2_ready, 3)
                    for c in range(KF):
                        ins = pe.matmul(ps[:, BANK_ATT[2], 2 * c:2 * c + 2], stage_a[:, c * P:(c + 1) * P],
                                        ones[:, 0:2], start=True, stop=True)
                    ins.then_inc(alpha_sum, 1)
                    transposes(0, xn2, xn2_ready, BANK_T2, t2_done)
                else:
                    pe.wait_ge(ffn_scaled, i - 1)
                    transposes(i - 1, xn2, xn2_ready, BANK_T2, t2_done)
                    A(i + 1)
                E(i - 1, 0)
                transposes(i + 1, xn1, xn1_ready, BANK_T1, t1_done)
                E(i - 1, 1)
                B(i + 1, i - 1)
                if at(i, 1):
                    pe.wait_ge(folded, 4)
                    pe.wait_ge(gate_ready, 3 * (i + 1) + 2)
                    pe.matmul(ps[:, BANK_FFN + 1, 0:DIM], ones[:, :], stage_b[:, 0:DIM], start=True,
                              stop=True).then_inc(alpha_sum, 1)
                D(i, i - 1)
                F(i - 1)

            steps(pe, body)
            n = NSEQ - 1
            transposes(n, xn2, xn2_ready, BANK_T2_LAST, t2_done)
            for part in range(len(parts(n))):
                E(n, part)
            F_last(n)


def chunked(a, k):
    import numpy as np
    return np.ascontiguousarray(a.reshape(k, P, a.shape[1]).transpose(1, 0, 2).reshape(P, k * a.shape[1]))


def kernel(x, L0_tok_W, L0_tok_b, L0_attn_Wi, L0_attn_conv_w, L0_attn_conv_b, L0_attn_Wg, L0_attn_bg,
           L0_attn_forget_base, L0_attn_Wo, L0_ffn_w1, L0_ffn_b1, L0_ffn_w2, L0_ffn_b2):
    import numpy as np
    import concourse.bacc as bacc
    from concourse.bass_utils import run_bass_kernel_spmd

    def cols(v):
        return np.asarray(v).reshape(-1, P).T

    conv_w = np.asarray(L0_attn_conv_w).reshape(KH, P, TAPS).transpose(1, 0, 2).reshape(P, KH * TAPS)
    arrays = {
        "xT": np.ascontiguousarray(np.asarray(x).reshape(NSEQ, T_IN, KX, P).transpose(0, 3, 2, 1)),
        "wtokT": chunked(np.asarray(L0_tok_W).T, NJ),
        "wiT": chunked(np.asarray(L0_attn_Wi).T, KX),
        "wgT": chunked(np.asarray(L0_attn_Wg).T, KH),
        "woT": chunked(np.asarray(L0_attn_Wo).T, KH),
        "w1T": chunked(np.asarray(L0_ffn_w1).T, KX),
        "w2T": chunked(np.asarray(L0_ffn_w2).T, KF),
        "params": np.ascontiguousarray(np.concatenate(
            [conv_w, cols(L0_attn_conv_b), cols(L0_attn_bg), cols(L0_attn_forget_base), cols(L0_ffn_b1)], axis=1)),
        "rows": np.ascontiguousarray(np.stack([np.asarray(L0_tok_b), np.asarray(L0_ffn_b2)])),
    }
    nc = bacc.Bacc("TRN2", target_bir_lowering=False, num_devices=1)
    args = [nc.dram_tensor(name, a.shape, F32, kind="ExternalInput").ap() for name, a in arrays.items()]
    out = nc.dram_tensor("out", (NSEQ, T, DIM), F32, kind="ExternalOutput").ap()
    tower(nc, *args, out.rearrange("s (t p) d -> s p t d", p=TT))
    r = run_bass_kernel_spmd(nc, [arrays], core_ids=[0])
    return r.results[0]["out"]
```

```python
from contextlib import ExitStack

import concourse.bass as bass
from concourse import mybir

ALU = mybir.AluOpType
ACT = mybir.ActivationFunctionType
F32 = mybir.dt.float32
F32R = mybir.dt.float32r

P = 128
NSEQ = 16
T_IN = 375
DIM = 256
SHIFTS = (0, 3, 6)
T = T_IN - SHIFTS[-1]
TP = T + 1
TT = 123
NT = T // TT
KX = DIM // P
HID = 384
KH = HID // P
FF = 1024
KF = FF // P
PART = ((0, 6), (6, 8))
LAST_PART = ((0, 2), (2, 4), (4, 6), (6, 8))
TAPS = 4
NJ = len(SHIFTS) * KX
LN_EPS = 1e-5
BETA_EPS = 1e-6
GATE_C = -8.0
S_CONVW, S_CONVB, S_BG, S_BASE, S_B1 = 0, 12, 15, 21, 24
S_COLS = 32
WARM_UP, KEEP_WARM = 11, 12
SP_STEPS = 20

BANK_FG = (7, 0, 1, 5, 6, 4)
BANK_FG_FIRST = (5, 6, 7, 0, 1, 4)
BANK_T2 = (2, 3)
BANK_TOK = (7, 0, 1)
BANK_E = (5, 6, 4, 2, 3, 1, 5, 6)
BANK_T1 = (7, 0)
BANK_T1_FIRST = (5, 6)
BANK_T1_SECOND = (2, 3)
BANK_ALPHA = (2, 3)
BANK_E_NEXT_LAST = (7, 0, 1, 2, 3, 5, 6, 4)
BANK_ATT_LAST = (7, 0, 1)
BANK_T2_LAST = (7, 0)
BANK_E_LAST = (6, 4, 1, 2, 3, 5, 6, 4)
BANK_FFN_LAST = {-2: (2, 3, 5), -1: (7, 0, 1)}
BANK_U = (7, 0, 1)
BANK_GATE = (2, 3, 4)
GATE_ORDER = (2, 0, 1)
BANK_ATT = (5, 6, 4)
BANK_FFN = 2


def need(eng, sem, value):
    if isinstance(value, int) and value <= 0:
        return
    eng.wait_ge(sem, value)


def parts(n):
    return LAST_PART if at(n, NSEQ - 2) or at(n, NSEQ - 1) else PART


def fg_banks(n):
    return BANK_FG_FIRST if at(n, 0) or at(n, 1) else BANK_FG


def e_banks(n):
    return BANK_E_NEXT_LAST if at(n, NSEQ - 2) else BANK_E_LAST if at(n, NSEQ - 1) else BANK_E


def at(i, k):
    return isinstance(i, int) and i == k


def tower(nc, xT, wtokT, wiT, wgT, woT, w1T, w2T, params, rows, out):
    with ExitStack() as ctx:
        def sb(name, shape, dt=F32):
            return ctx.enter_context(nc.sbuf_tensor(name, shape, dt))

        def sem(name):
            return ctx.enter_context(nc.semaphore(name))

        ps = ctx.enter_context(nc.psum_tensor("ps", [P, 8, 512], F32))

        tok_wh, tok_wl = sb("tok_wh", [P, NJ, DIM], F32R), sb("tok_wl", [P, NJ, DIM], F32R)
        wi_h, wi_l = sb("wi_h", [P, KX, 2 * HID], F32R), sb("wi_l", [P, KX, 2 * HID], F32R)
        wg_h, wg_l = sb("wg_h", [P, KH, 2 * HID], F32R), sb("wg_l", [P, KH, 2 * HID], F32R)
        wo_h, wo_l = sb("wo_h", [P, KH, DIM], F32R), sb("wo_l", [P, KH, DIM], F32R)
        w1_sign = sb("w1_sign", [P, KX, FF], F32R)
        w2_sign = sb("w2_sign", [P, KF, DIM], F32R)
        stage_a, stage_b = sb("stage_a", [P, 2048]), sb("stage_b", [P, 2048])
        par = sb("par", [P, S_COLS])
        row = sb("row", [P, 2, DIM])
        alpha1 = sb("alpha1", [P, KF])
        alpha2 = sb("alpha2", [P, DIM])
        half_bg = sb("half_bg", [P, 2 * KH])
        decay_c = sb("decay_c", [P, KH])
        sp = sb("sp", [P, 6, KH])
        ident = sb("ident", [P, P])
        ones = sb("ones", [P, P])
        mhalf = sb("mhalf", [P, NT])
        ln_bias = sb("ln_bias", [P, 1])

        tok_raw = stage_a[:, 0:NJ * DIM].rearrange("p (j o) -> p j o", j=NJ)

        x_raw = sb("x_raw", [P, 2, KX, T_IN])
        x_h, x_l = sb("x_h", [P, KX, T_IN], F32R), sb("x_l", [P, KX, T_IN], F32R)
        h = sb("h", [P, 2, NT, DIM])
        outb = sb("outb", [P, 2, NT, DIM])
        ffn_s = sb("ffn_s", [P, NT, DIM])
        xn1, xn2 = sb("xn1", [P, NT, DIM]), sb("xn2", [P, NT, DIM])
        stats = [sb(f"stats{j}", [P, NT, 6]) for j in (0, 1)]
        moment = [sb(f"moment{j}", [P, NT, 5]) for j in (0, 1)]
        mean = [sb(f"mean{j}", [P, NT]) for j in (0, 1)]
        var_eps = [sb(f"var_eps{j}", [P, NT]) for j in (0, 1)]
        rstd = [sb(f"rstd{j}", [P, NT]) for j in (0, 1)]
        xa_h, xa_l = sb("xa_h", [P, KX, TP], F32R), sb("xa_l", [P, KX, TP], F32R)
        xb_h, xb_l = sb("xb_h", [P, KX, TP], F32R), sb("xb_l", [P, KX, TP], F32R)
        uc = sb("uc", [P, KH, T])
        u_h, u_l = sb("u_h", [P, KH, TP], F32R), sb("u_l", [P, KH, TP], F32R)
        x1_h, x1_l = (u[:, :, :].rearrange("p a b -> p (a b)")[:, 0:KX * T_IN].rearrange("p (a b) -> p a b", a=KX)
                      for u in (u_h, u_l))
        gate = sb("gate", [P, 2, KH, T])
        decay = sb("decay", [P, KH, T])
        beta = sb("beta", [P, KH, T])
        state = sb("state", [P, KH, T])
        y_h, y_l = sb("y_h", [P, KH, T], F32R), sb("y_l", [P, KH, T], F32R)
        g = sb("g", [P, KF, T])
        stage_c = g[:, :, :].rearrange("p a b -> p (a b)")[:, 0:KH * 2 * HID]
        g_h, g_l = sb("g_h", [P, KF, T], F32R), sb("g_l", [P, KF, T], F32R)

        in_x = [sem("in_x0"), sem("in_x1")]
        in_tok = [sem("in_tok0"), sem("in_tok1")]
        in_wi, in_wg, in_wo = sem("in_wi"), sem("in_wg"), sem("in_wo")
        in_w1, in_w2, in_par, in_row = sem("in_w1"), sem("in_w2"), sem("in_par"), sem("in_row")
        out_stored = [sem("out_stored0"), sem("out_stored1")]
        consts_ready, ident_zero, ident_ready, pads_ready = (
            sem("consts_ready"), sem("ident_zero"), sem("ident_ready"), sem("pads_ready"))
        w_hi, w_lo, wi_lo, wg_lo = sem("w_hi"), sem("w_lo"), sem("wi_lo"), sem("wg_lo")
        sp_step, sp_exp = sem("sp_step"), sem("sp_exp")
        sign_part, signs_ready, w2_step = sem("sign_part"), sem("signs_ready"), sem("w2_step")
        g_lo_pool = sem("g_lo_pool")
        g_hi_last = sem("g_hi_last")
        folded = sem("folded")
        abs_ready, alpha_sum, alpha_ready = sem("abs_ready"), sem("alpha_sum"), sem("alpha_ready")
        x_hi, x_split = sem("x_hi"), sem("x_split")
        tok_done, h_ready = sem("tok_done"), sem("h_ready")
        bn_ready = [sem("bn_ready1"), sem("bn_ready2")]
        sums_ready, terms_ready = [sem("sums1"), sem("sums2")], [sem("terms1"), sem("terms2")]
        veps_ready, rstd_ready = [sem("veps1"), sem("veps2")], [sem("rstd1"), sem("rstd2")]
        xn1_ready, t1_done, xa_hi, xa_lo = sem("xn1_ready"), sem("t1_done"), sem("xa_hi"), sem("xa_lo")
        gi_done = sem("gi_done")
        tap0_ready, taps, u_hi, u_lo = sem("tap0_ready"), sem("taps"), sem("u_hi"), sem("u_lo")
        gate_ready = sem("gate_ready")
        fg_done, tanh_ready = sem("fg_done"), sem("tanh_ready")
        decay_ready, sq_ready, ln_ready, beta_ready = (
            sem("decay_ready"), sem("sq_ready"), sem("ln_ready"), sem("beta_ready"))
        v_ready, xt_ready, scanned, y_ready, y_hi, y_lo = (
            sem("v_ready"), sem("xt_ready"), sem("scanned"), sem("y_ready"), sem("y_hi"), sem("y_lo"))
        att_done, h2_ready = sem("att_done"), sem("h2_ready")
        xn2_ready, t2_done, xb_hi, xb_lo = sem("xn2_ready"), sem("t2_done"), sem("xb_hi"), sem("xb_lo")
        ff1_done, g_ready, g_hi, g_lo = sem("ff1_done"), sem("g_ready"), sem("g_hi"), sem("g_lo")
        ffn_done, ffn_scaled, outb_ready, out_ready = (
            sem("ffn_done"), sem("ffn_scaled"), sem("outb_ready"), sem("out_ready"))

        def raw(a):
            return a.bitcast(F32)

        def steps(eng, body):
            for i in (0, 1):
                body(i, i % 2)
            with eng.Fori(1, NSEQ // 2 - 1) as pair:
                body(2 * pair, 0)
                body(2 * pair + 1, 1)
            for i in (NSEQ - 2, NSEQ - 1):
                body(i, i % 2)

        def ffn_tile(n, t):
            if at(n, NSEQ - 2) or at(n, NSEQ - 1):
                return ps[0:TT, BANK_FFN_LAST[n - NSEQ][t], 0:DIM]
            return ps[0:TT, BANK_FFN:BANK_FFN + 2].rearrange("p b n -> p (b n)")[:, t * DIM:(t + 1) * DIM]

        def exists(i):
            return not isinstance(i, int) or 0 <= i < NSEQ

        block = ctx.enter_context(nc.Block())

        @block.sync
        def _(sp_eng):
            def load(n, p):
                need(sp_eng, x_split, n - 1)
                sp_eng.dma_start(x_raw[:, p], xT[n]).then_inc(in_x[p], 16)

            def store(n, p):
                need(sp_eng, out_ready, n + 1)
                sp_eng.dma_start(out[n], outb[0:TT, p]).then_inc(out_stored[p], 16)

            def store_tiles(n, p):
                for t in range(NT):
                    sp_eng.wait_ge(out_ready, n + 1 + t)
                    sp_eng.dma_start(out[n][:, t], outb[0:TT, p, t]).then_inc(out_stored[p], 16)

            load(0, 0)
            for k in (0, 1):
                cols = slice(k * NJ // 2 * DIM, (k + 1) * NJ // 2 * DIM)
                sp_eng.dma_start(stage_a[:, cols], wtokT[:, cols]).then_inc(in_tok[k], 16)
            load(1, 1)
            sp_eng.dma_start(stage_b[:, 0:KX * 2 * HID], wiT).then_inc(in_wi, 16)
            sp_eng.dma_start(stage_c[:, :], wgT).then_inc(in_wg, 16)
            sp_eng.wait_ge(w_hi, 2)
            sp_eng.wait_ge(w_lo, 2)
            sp_eng.dma_start(stage_a[:, :], w1T).then_inc(in_w1, 16)
            sp_eng.wait_ge(w_hi, 4)
            sp_eng.wait_ge(wi_lo, 1)
            sp_eng.dma_start(stage_b[:, :], w2T).then_inc(in_w2, 16)
            sp_eng.wait_ge(wg_lo, KH)
            sp_eng.dma_start(stage_c[:, 0:KH * DIM], woT).then_inc(in_wo, 16)

            def body(i, p):
                if exists(i + 2):
                    load(i + 2, p)
                if exists(i - 1):
                    store(i - 1, 1 - p)

            steps(sp_eng, body)
            store_tiles(NSEQ - 1, (NSEQ - 1) % 2)
            sp_eng.wait_ge(out_stored[0], 16 * (NSEQ // 2))
            sp_eng.wait_ge(out_stored[1], 16 * (NSEQ // 2 - 1 + NT))

        @block.gpsimd
        def _(pool):
            pool.memset(ident[:, :], 0.0).then_inc(ident_zero, 1)
            pool.memset(ones[:, :], 1.0).then_inc(consts_ready, 1)
            pool.memset(mhalf[:, :], -0.5).then_inc(consts_ready, 1)
            pool.memset(ln_bias[:, :], 0.25 * (1.0 + BETA_EPS)).then_inc(consts_ready, 1)
            for padded in (xa_h, xa_l, xb_h, xb_l):
                pool.memset(raw(padded[:, :, T:TP]), 0.0).then_inc(pads_ready, 1)
            pool.wait_ge(ident_zero, 1)
            pool.affine_select(out=ident[:, :], in_=ident[:, :], compare_op=ALU.not_equal, fill=1.0, base=0,
                               pattern=[[-1, P]], channel_multiplier=1).then_inc(ident_ready, 1)
            pool.wait_ge(consts_ready, 3)

            def split_x(n, p):
                pool.wait_ge(x_hi, n + 1)
                hi, lo = (x1_h, x1_l) if at(n, 1) else (x_h[:, :, :], x_l[:, :, :])
                pool.tensor_tensor(lo, x_raw[:, p], raw(hi), ALU.subtract).then_inc(x_split, 1)

            def rsqrt(n, which):
                pool.wait_ge(veps_ready[which], n + 1)
                pool.tensor_tensor(rstd[which][0:TT, :], var_eps[which][0:TT, :], mhalf[0:TT, :],
                                   ALU.pow).then_inc(rstd_ready[which], 1)

            def residual(n, p):
                if at(n, 0):
                    pool.wait_ge(h2_ready, NT)
                else:
                    rsqrt(n, 1)
                if not at(n, 0) and not at(n, 1):
                    pool.wait_ge(out_stored[p], 8 * (n - p))
                for t in range(NT):
                    ins = pool.tensor_tensor(outb[0:TT, p, t], h[0:TT, p, t], row[0:TT, 1], ALU.add)
                ins.then_inc(outb_ready, 1)
                if at(n, 0):
                    rsqrt(0, 1)

            def w2_signs():
                flat_sign = w2_sign[:, :, :].rearrange("p a b -> p (a b)")
                positive = g_h[:, :, :].rearrange("p a b -> p (a b)")[:, 0:KF * DIM]
                pool.wait_ge(in_w2, 16)
                pool.tensor_scalar(flat_sign, stage_b[:, :], 0.0, None, ALU.is_lt).then_inc(w2_step, 1)
                pool.tensor_scalar(positive, stage_b[:, :], 0.0, None, ALU.is_gt).then_inc(w2_step, 1)
                pool.wait_ge(w2_step, 2)
                pool.tensor_tensor(flat_sign, raw(positive), raw(flat_sign), ALU.subtract).then_inc(w2_step, 1)
                pool.wait_ge(w2_step, 3)
                pool.tensor_tensor(stage_b[:, :], stage_b[:, :], raw(flat_sign), ALU.mult).then_inc(w2_step, 1)
                pool.wait_ge(w2_step, 4)

            def fold_w2():
                half = KF * DIM // 2
                for k in range(3):
                    pool.tensor_tensor(stage_b[:, 0:half], stage_b[:, 0:half], stage_b[:, half:2 * half],
                                       ALU.add).then_inc(folded, 1)
                    pool.wait_ge(folded, k + 1)
                    half //= 2

            def fold_w1():
                pool.wait_ge(abs_ready, 1)
                pool.tensor_tensor(stage_a[:, 0:FF], stage_a[:, 0:FF], stage_a[:, FF:2 * FF],
                                   ALU.add).then_inc(folded, 1)

            def ffn_low_pool(part):
                n = NSEQ - 2
                a, b = parts(n)[part]
                pool.wait_ge(g_hi, 2 * n + part + 1)
                pool.tensor_tensor(g_l[:, a:b], g[:, a:b], raw(g_h[:, a:b]), ALU.subtract).then_inc(g_lo_pool, 1)

            def body(i, p):
                if at(i, 1):
                    residual(0, 0)
                if at(i, NSEQ - 1):
                    ffn_low_pool(0)
                    ffn_low_pool(1)
                if exists(i + 1) and not at(i, 0):
                    rsqrt(i + 1, 0)
                if exists(i + 2):
                    split_x(i + 2, p)
                if not at(i, 0):
                    residual(i, p)
                if exists(i - 1):
                    finish(i - 1, 1 - p)

            def finish(n, p):
                pool.wait_ge(outb_ready, n + 1)
                pool.wait_ge(ffn_scaled, n + 1)
                pool.tensor_tensor(outb[0:TT, p], outb[0:TT, p], ffn_s[0:TT], ALU.add).then_inc(out_ready, 1)

            def wg_low(k):
                pool.wait_ge(w_hi, 4)
                pool.tensor_tensor(wg_l[:, k], stage_c[:, k * 2 * HID:(k + 1) * 2 * HID], raw(wg_h[:, k]),
                                   ALU.subtract).then_inc(wg_lo, 1)

            split_x(0, 0)
            split_x(1, 1)
            pool.wait_ge(w_hi, 3)
            pool.tensor_tensor(wi_l[:, :, :].rearrange("p a b -> p (a b)"), stage_b[:, 0:KX * 2 * HID],
                               raw(wi_h[:, :, :]).rearrange("p a b -> p (a b)"), ALU.subtract).then_inc(wi_lo, 1)
            rsqrt(0, 0)
            wg_low(0)
            wg_low(1)
            wg_low(2)
            pool.wait_ge(tok_done, 6)
            for padded in (u_h, u_l):
                pool.memset(raw(padded[:, :, T:TP]), 0.0).then_inc(pads_ready, 1)
            rsqrt(1, 0)
            w2_signs()
            fold_w2()
            fold_w1()
            pool.wait_ge(in_row, 16)
            steps(pool, body)

        @block.scalar
        def _(act):
            act.dma_start(par[:, :], params).then_inc(in_par, 16)
            act.dma_start(row[:, :, :], rows.partition_broadcast(P)).then_inc(in_row, 16)

            act.wait_ge(sp_step, 2)
            act.activation(sp[:, 2], sp[:, 1], ACT.Exp, scale=-1.0).then_inc(sp_exp, 1)

            def hi_part(dst, src, arrived):
                act.wait_ge(arrived, 16)
                act.activation(dst, src, ACT.Copy).then_inc(w_hi, 1)

            def w1_magnitudes():
                act.wait_ge(signs_ready, 1)
                act.activation(stage_a[:, :], stage_a[:, :], ACT.Abs).then_inc(abs_ready, 1)

            def x_part(n, p):
                act.wait_ge(in_x[p], 8 * (n - p) + 16)
                if not at(n, 1):
                    need(act, tok_done, 3 * n)
                dst = x1_h if at(n, 1) else x_h[:, :, :]
                act.activation(dst, x_raw[:, p], ACT.Copy).then_inc(x_hi, 1)

            x_part(0, 0)
            for k in (0, 1):
                js = slice(k * NJ // 2, (k + 1) * NJ // 2)
                hi_part(tok_wh[:, js], tok_raw[:, js], in_tok[k])
            x_part(1, 1)
            hi_part(wi_h[:, :, :].rearrange("p a b -> p (a b)"), stage_b[:, 0:KX * 2 * HID], in_wi)
            hi_part(wg_h[:, :, :].rearrange("p a b -> p (a b)"), stage_c[:, :], in_wg)

            def xa_parts(n, banks):
                for c in range(KX):
                    act.wait_ge(t1_done, 2 * n + c + 1)
                    if c == 0:
                        need(act, gi_done, 6 * n)
                    act.activation(xa_h[:, c, 0:T], ps[:, banks[c], 0:T], ACT.Copy).then_inc(xa_hi, 1)

            def last_tap(n, chunks=range(KH)):
                for c in chunks:
                    act.wait_ge(gi_done, 6 * n + c + 1)
                    if c == 0:
                        need(act, v_ready, n)
                        need(act, u_lo, 3 * n)
                    act.activation(uc[:, c], ps[:, BANK_U[c], 0:T], ACT.Identity,
                                   scale=par[:, S_CONVW + TAPS * c + 3:S_CONVW + TAPS * c + 4],
                                   bias=par[:, S_CONVB + c:S_CONVB + c + 1]).then_inc(tap0_ready, 1)

            def gate_gelu(n, p, chunks=GATE_ORDER):
                act.wait_ge(gi_done, 6 * n + 2 * KH)
                need(act, y_ready, n - 1)
                for c in chunks:
                    act.activation(gate[:, p, c], ps[:, BANK_GATE[c], 0:T], ACT.Gelu).then_inc(gate_ready, 1)

            def u_parts(n, chunks=range(KH)):
                need(act, fg_done, 6 * n)
                for c in chunks:
                    act.wait_ge(taps, 9 * n + 3 * (c + 1) if at(n, 0) or at(n, 1) else 9 * n + 6 + c + 1)
                    act.activation(u_h[:, c, 0:T], uc[:, c], ACT.Copy).then_inc(u_hi, 1)

            def gates_tanh(n, ms=range(2 * KH)):
                for m in ms:
                    act.wait_ge(fg_done, 6 * n + m + 1)
                    if m == 0:
                        need(act, scanned, 3 * n)
                    if m == KH:
                        need(act, y_lo, n)
                    dst = decay[:, m] if m < KH else state[:, m - KH]
                    act.activation(dst, ps[:, fg_banks(n)[m], 0:T], ACT.Tanh, scale=0.5,
                                   bias=half_bg[:, m:m + 1]).then_inc(tanh_ready, 1)

            def xb_parts(n, banks=BANK_T2):
                for c in range(KX):
                    act.wait_ge(t2_done, 2 * n + c + 1)
                    if c == 0:
                        need(act, ff1_done, 8 * n)
                    act.activation(xb_h[:, c, 0:T], ps[:, banks[c], 0:T], ACT.Copy).then_inc(xb_hi, 1)

            def decays(n):
                act.preload_act_table_set("natural_log_exp_and_others")
                for c in range(KH):
                    if at(n, 0):
                        last_tap(1, [c])
                    act.wait_ge(tanh_ready, 6 * n + c + 1)
                    act.activation(decay[:, c], decay[:, c], ACT.Exp, scale=decay_c[:, c:c + 1],
                                   bias=decay_c[:, c:c + 1]).then_inc(decay_ready, 1)
                if at(n, 0):
                    u_parts(1, range(0, 2))
                if at(n, NSEQ - 1):
                    xb_parts(n - 1)
                else:
                    act.wait_ge(decay_ready, 3 * n + 3)
                    need(act, xt_ready, n)
                    act.activation(beta[:, :, :], decay[:, :, :], ACT.Square).then_inc(sq_ready, 1)
                if at(n, 0):
                    u_parts(1, range(2, 3))
                act.wait_ge(sq_ready, n + 1)
                act.activation(beta[:, :, :], beta[:, :, :], ACT.Ln, scale=-0.25,
                               bias=ln_bias[:, 0:1]).then_inc(ln_ready, 1)
                act.wait_ge(ln_ready, n + 1)
                act.activation(beta[:, :, :], beta[:, :, :], ACT.Exp, scale=0.5).then_inc(beta_ready, 1)

            def ffn_gelu(n, half, chunks=None):
                for c in chunks or range(*parts(n)[half]):
                    act.wait_ge(ff1_done, 8 * n + c + 1)
                    if c == parts(n)[half][0]:
                        need(act, g_lo, 2 * n if len(parts(n)) > 2 else 2 * n - 1 + half)
                        if at(n, NSEQ - 1):
                            act.wait_ge(g_lo_pool, 2)
                    act.activation(g[:, c], ps[:, e_banks(n)[c], 0:T], ACT.Gelu, scale=alpha1[:, c:c + 1],
                                   bias=par[:, S_B1 + c:S_B1 + c + 1]).then_inc(g_ready, 1)

            def ffn_hi(n, half):
                a, b = parts(n)[half]
                act.wait_ge(g_ready, 8 * n + b)
                need(act, ffn_done, n)
                act.activation(g_h[:, a:b], g[:, a:b],
                               ACT.Copy).then_inc(g_hi, 1)

            def y_part_chunk(n, c):
                act.wait_ge(y_ready, n + 1 + c)
                if c == 0:
                    act.wait_ge(att_done, 3 * n)
                act.activation(y_h[:, c], state[:, c], ACT.Copy).then_inc(y_hi, 1)

            def y_part(n):
                act.wait_ge(y_ready, n + 1)
                need(act, att_done, 3 * n)
                act.activation(y_h[:, :, :], state[:, :, :], ACT.Copy).then_inc(y_hi, 1)

            act.wait_ge(in_par, 16)
            xa_parts(0, BANK_T1_FIRST)
            last_tap(0)
            u_parts(0)
            gate_gelu(0, 0)
            hi_part(wo_h[:, :, :].rearrange("p a b -> p (a b)"), stage_c[:, 0:KH * DIM], in_wo)

            def first(i, p):
                gates_tanh(0, range(KH))
                xa_parts(1, BANK_T1_SECOND)
                w1_magnitudes()
                gates_tanh(0, range(KH, 2 * KH))
                act.wait_ge(sp_step, SP_STEPS)
                decays(0)
                gate_gelu(1, 1)
                y_part(0)
                x_part(2, 0)

            def last(i, p):
                n = NSEQ - 1
                gates_tanh(n, range(KH))
                decays(n)
                act.preload_act_table_set("gelu_and_others")
                gates_tanh(n, range(KH, 2 * KH))
                ffn_gelu(n - 1, 0)
                ffn_hi(n - 1, 0)
                ffn_gelu(n - 1, 1, [2])
                y_part_chunk(n, 0)
                ffn_gelu(n - 1, 1, [3])
                y_part_chunk(n, 1)
                ffn_hi(n - 1, 1)
                y_part_chunk(n, 2)
                for part in (2, 3):
                    ffn_gelu(n - 1, part)
                    ffn_hi(n - 1, part)

            def body(i, p):
                if at(i, 0):
                    return first(i, p)
                if at(i, NSEQ - 1):
                    return last(i, p)
                gates_tanh(i)
                if at(i, 1):
                    decays(i)
                    xb_parts(i - 1)
                    act.wait_ge(w_lo, 3)
                    act.wait_ge(alpha_ready, 1)
                else:
                    xb_parts(i - 1)
                    decays(i)
                ffn_gelu(i - 1, 0, range(0, 3))
                xa_parts(i + 1, BANK_T1)
                ffn_gelu(i - 1, 0, range(3, 6))
                ffn_gelu(i - 1, 1)
                y_part(i)
                ffn_hi(i - 1, 0)
                gate_gelu(i + 1, 1 - p, GATE_ORDER[:1])
                last_tap(i + 1)
                gate_gelu(i + 1, 1 - p, GATE_ORDER[1:])
                ffn_hi(i - 1, 1)
                if exists(i + 2):
                    x_part(i + 2, p)
                u_parts(i + 1)

            steps(act, body)
            n = NSEQ - 1
            xb_parts(n, BANK_T2_LAST)
            for part in range(len(parts(n))):
                ffn_gelu(n, part)
                if part in (0, 3):
                    ffn_hi(n, part)

        @block.vector
        def _(dve):
            step = [0]

            def sp_op(ins):
                step[0] += 1
                ins.then_inc(sp_step, 1)
                dve.wait_ge(sp_step, step[0])

            dve.wait_ge(in_par, 16)
            base = par[:, S_BASE:S_BASE + KH]
            sp_op(dve.tensor_scalar(sp[:, 0], base, -1.0, None, ALU.mult))
            sp_op(dve.tensor_tensor(sp[:, 1], base, sp[:, 0], ALU.max))
            sp_op(dve.tensor_scalar(half_bg[:, :], par[:, S_BG:S_BG + 2 * KH], 0.5, None, ALU.mult))

            def softplus():
                dve.wait_ge(sp_exp, 1)
                sp_op(dve.tensor_scalar(sp[:, 3], sp[:, 2], 2.0, None, ALU.add))
                sp_op(dve.reciprocal(sp[:, 4], sp[:, 3]))
                sp_op(dve.tensor_tensor(sp[:, 2], sp[:, 2], sp[:, 4], ALU.mult))
                sp_op(dve.tensor_tensor(sp[:, 3], sp[:, 2], sp[:, 2], ALU.mult))
                last = 9
                for k in range(last, 0, -1):
                    src = sp[:, 4] if k < last else sp[:, 5]
                    if k == last:
                        ins = dve.memset(sp[:, 5], 0.0)
                        ins.then_inc(sp_step, 1)
                        step[0] += 1
                        dve.wait_ge(sp_step, step[0])
                    sp_op(dve.scalar_tensor_tensor(out=sp[:, 4], in0=src, scalar=1.0 / (2 * k + 1), in1=sp[:, 3],
                                                   op0=ALU.add, op1=ALU.mult))
                sp_op(dve.scalar_tensor_tensor(out=sp[:, 4], in0=sp[:, 4], scalar=1.0, in1=sp[:, 2],
                                               op0=ALU.add, op1=ALU.mult))
                sp_op(dve.tensor_scalar(sp[:, 0], base, 0.0, 0.5 * GATE_C, ALU.max, ALU.mult))
                sp_op(dve.scalar_tensor_tensor(out=decay_c[:, :], in0=sp[:, 4], scalar=GATE_C, in1=sp[:, 0],
                                               op0=ALU.mult, op1=ALU.add))
                assert step[0] == SP_STEPS

            def lo_part(k, dst, src, hi):
                dve.wait_ge(w_hi, k)
                dve.tensor_tensor(dst, src, raw(hi), ALU.subtract).then_inc(w_lo, 1)

            def flat(a):
                return a[:, :, :].rearrange("p a b -> p (a b)")

            for k in (0, 1):
                js = slice(k * NJ // 2, (k + 1) * NJ // 2)
                lo_part(k + 1, tok_wl[:, js], tok_raw[:, js], tok_wh[:, js])
            def w1_signs():
                dve.wait_ge(in_w1, 16)
                dve.tensor_scalar(flat(w1_sign), stage_a[:, :], 0.0, None, ALU.is_lt).then_inc(sign_part, 1)
                dve.wait_ge(sign_part, 1)
                dve.scalar_tensor_tensor(out=flat(w1_sign), in0=stage_a[:, :], scalar=0.0, in1=raw(flat(w1_sign)),
                                         op0=ALU.is_gt, op1=ALU.subtract).then_inc(signs_ready, 1)

            def add_tok(n, p, tiles=range(NT)):
                for t in tiles:
                    dve.wait_ge(tok_done, 3 * n + t + 1)
                    if t == 0:
                        need(dve, outb_ready, n - 1)
                    dve.tensor_tensor(h[0:TT, p, t], ps[0:TT, BANK_TOK[t], 0:DIM], row[0:TT, 0],
                                      ALU.add).then_inc(h_ready, 1)
                    dve.wait_ge(h_ready, 3 * n + t + 1)
                    dve.bn_stats(stats[0][0:TT, t], h[0:TT, p, t]).then_inc(bn_ready[0], 1)

            def moments(n, which):
                st, mo = stats[which][0:TT], moment[which]
                dve.wait_ge(bn_ready[which], 3 * n + 3)
                dve.tensor_tensor(mo[0:TT, :, 0:2], st[:, :, 1:3], st[:, :, 4:6], ALU.add).then_inc(sums_ready[which], 1)
                dve.tensor_tensor(mo[0:TT, :, 2], st[:, :, 1], st[:, :, 4], ALU.subtract).then_inc(sums_ready[which], 1)
                dve.wait_ge(sums_ready[which], 2 * n + 2)
                dve.tensor_scalar(mo[0:TT, :, 3], mo[0:TT, :, 1], 1.0 / DIM, LN_EPS, ALU.mult,
                                  ALU.add).then_inc(terms_ready[which], 1)
                dve.scalar_tensor_tensor(out=mo[0:TT, :, 4], in0=mo[0:TT, :, 2], scalar=0.25, in1=mo[0:TT, :, 2],
                                         op0=ALU.mult, op1=ALU.mult).then_inc(terms_ready[which], 1)
                dve.tensor_scalar(mean[which][0:TT, :], mo[0:TT, :, 0], 0.5, None, ALU.mult).then_inc(
                    terms_ready[which], 1)
                dve.wait_ge(terms_ready[which], 3 * n + 3)
                dve.tensor_tensor(var_eps[which][0:TT, :], mo[0:TT, :, 3], mo[0:TT, :, 4], ALU.add).then_inc(
                    veps_ready[which], 1)

            def norm(n, p, which, xn, ready, transposed):
                dve.wait_ge(rstd_ready[which], n + 1)
                need(dve, transposed, 2 * n)
                for t in range(NT):
                    dve.tensor_scalar(xn[0:TT, t], h[0:TT, p, t], mean[which][0:TT, t:t + 1],
                                      rstd[which][0:TT, t:t + 1], ALU.subtract, ALU.mult).then_inc(ready, 1)

            def xa_low(n, banks):
                for c in range(KX):
                    dve.wait_ge(xa_hi, 2 * n + c + 1)
                    dve.tensor_tensor(xa_l[:, c, 0:T], ps[:, banks[c], 0:T], raw(xa_h[:, c, 0:T]),
                                      ALU.subtract).then_inc(xa_lo, 1)

            def conv(n, delays):
                for d in delays:
                    for c in range(KH):
                        if d == 1:
                            dve.wait_ge(tap0_ready, 3 * n + c + 1)
                        else:
                            dve.wait_ge(taps, 9 * n + 3 * (d - 2) + c + 1)
                        tap(c, d)

            def tap(c, d):
                w = S_CONVW + TAPS * c + 3 - d
                dve.scalar_tensor_tensor(out=uc[:, c, d:T], in0=ps[:, BANK_U[c], 0:T - d],
                                         scalar=par[:, w:w + 1], in1=uc[:, c, d:T],
                                         op0=ALU.mult, op1=ALU.add).then_inc(taps, 1)

            def conv_by_chunk(n):
                for c in range(KH):
                    if c == 2:
                        u_low(n, [0])
                    for d in range(1, TAPS):
                        if d == 1:
                            dve.wait_ge(tap0_ready, 3 * n + c + 1)
                        else:
                            dve.wait_ge(taps, 9 * n + 3 * c + d - 1)
                        tap(c, d)
                u_low(n, [1, 2])

            def u_low(n, chunks=range(KH)):
                for c in chunks:
                    dve.wait_ge(u_hi, 3 * n + c + 1)
                    dve.tensor_tensor(u_l[:, c, 0:T], uc[:, c], raw(u_h[:, c, 0:T]), ALU.subtract).then_inc(u_lo, 1)

            def input_term(n):
                dve.wait_ge(tanh_ready, 6 * n + 6)
                dve.scalar_tensor_tensor(out=state[:, :, :], in0=state[:, :, :], scalar=1.0, in1=uc[:, :, :],
                                         op0=ALU.add, op1=ALU.mult).then_inc(v_ready, 1)

            def xb_low(n, banks=BANK_T2):
                for c in range(KX):
                    dve.wait_ge(xb_hi, 2 * n + c + 1)
                    dve.tensor_tensor(xb_l[:, c, 0:T], ps[:, banks[c], 0:T], raw(xb_h[:, c, 0:T]),
                                      ALU.subtract).then_inc(xb_lo, 1)

            def scale_input(n, a=0, b=KH):
                if a == 0:
                    dve.wait_ge(v_ready, n + 1)
                    dve.wait_ge(beta_ready, n + 1)
                ins = dve.tensor_tensor(state[:, a:b], state[:, a:b], beta[:, a:b], ALU.mult)
                if b == KH:
                    ins.then_inc(xt_ready, 1)

            def recur(n, chunks=range(KH)):
                dve.wait_ge(xt_ready, n + 1)
                for c in chunks:
                    dve.tensor_tensor_scan(state[:, c], decay[:, c], state[:, c], 0.0, ALU.mult,
                                           ALU.add).then_inc(scanned, 1)

            def gated(n, p):
                dve.wait_ge(scanned, 3 * n + 3)
                dve.wait_ge(gate_ready, 3 * n + 3)
                dve.tensor_tensor(state[:, :, :], state[:, :, :], gate[:, p], ALU.mult).then_inc(y_ready, 1)

            def y_low(n):
                dve.wait_ge(y_hi, n + 1)
                dve.tensor_tensor(y_l[:, :, :], state[:, :, :], raw(y_h[:, :, :]), ALU.subtract).then_inc(y_lo, 1)

            def ffn_low(n, half):
                a, b = parts(n)[half]
                if at(n, NSEQ - 1) and half in (1, 2):
                    dve.wait_ge(g_hi_last, half)
                elif at(n, NSEQ - 1):
                    dve.wait_ge(g_hi, 2 * (n + 1) + (1 if half == 0 else 2))
                else:
                    dve.wait_ge(g_hi, 2 * n + half + 1)
                dve.tensor_tensor(g_l[:, a:b], g[:, a:b], raw(g_h[:, a:b]), ALU.subtract).then_inc(g_lo, 1)

            def add_att(n, p):
                banks = BANK_ATT_LAST if at(n, NSEQ - 1) else BANK_ATT
                for t in range(NT):
                    dve.wait_ge(att_done, 3 * n + t + 1)
                    dve.tensor_tensor(h[0:TT, p, t], h[0:TT, p, t], ps[0:TT, banks[t], 0:DIM],
                                      ALU.add).then_inc(h2_ready, 1)
                for t in range(NT):
                    dve.wait_ge(h2_ready, 3 * n + t + 1)
                    dve.bn_stats(stats[1][0:TT, t], h[0:TT, p, t]).then_inc(bn_ready[1], 1)
                moments(n, 1)

            def scale_ffn(n):
                dve.wait_ge(ffn_done, n + 1)
                need(dve, out_ready, n)
                for t in range(NT):
                    ins = dve.tensor_tensor(ffn_s[0:TT, t], ffn_tile(n, t), alpha2[0:TT, :], ALU.mult)
                ins.then_inc(ffn_scaled, 1)

            softplus()
            dve.wait_ge(in_row, 16)
            add_tok(0, 0)
            moments(0, 0)
            norm(0, 0, 0, xn1, xn1_ready, t1_done)
            add_tok(1, 1, (0, 1))
            xa_low(0, BANK_T1_FIRST)
            add_tok(1, 1, (2,))
            moments(1, 0)
            conv_by_chunk(0)
            norm(1, 1, 0, xn1, xn1_ready, t1_done)
            w1_signs()
            xa_low(1, BANK_T1_SECOND)
            lo_part(5, flat(wo_l), stage_c[:, 0:KH * DIM], flat(wo_h))

            def first(i, p):
                input_term(0)
                conv_by_chunk(1)
                scale_input(0)
                recur(0)
                gated(0, 0)
                y_low(0)
                dve.wait_ge(alpha_sum, 1)
                dve.tensor_scalar(alpha1[:, :], ps[:, BANK_ALPHA[0], 0:2 * KF:2], 1.0 / DIM, None,
                                  ALU.mult).then_inc(alpha_ready, 1)
                dve.wait_ge(alpha_sum, 2)
                dve.tensor_scalar(alpha2[:, :], ps[:, BANK_ALPHA[1], 0:DIM], 1.0 / FF, None,
                                  ALU.mult).then_inc(alpha_ready, 1)

            def last(i, p):
                n = NSEQ - 1
                for c in range(KH):
                    dve.wait_ge(decay_ready, 3 * n + c + 1)
                    ins = dve.tensor_tensor(beta[:, c], decay[:, c], decay[:, c], ALU.mult)
                ins.then_inc(sq_ready, 1)
                xb_low(n - 1)

                def input_chunk(c):
                    dve.wait_ge(tanh_ready, 6 * n + KH + c + 1)
                    dve.scalar_tensor_tensor(out=state[:, c], in0=state[:, c], scalar=1.0, in1=uc[:, c],
                                             op0=ALU.add, op1=ALU.mult).then_inc(v_ready, 1)

                def scale_chunk(c):
                    if c == 0:
                        dve.wait_ge(beta_ready, n + 1)
                    dve.wait_ge(v_ready, n + 1 + c)
                    dve.tensor_tensor(state[:, c], state[:, c], beta[:, c], ALU.mult).then_inc(xt_ready, 1)

                def scan_chunk(c):
                    dve.wait_ge(xt_ready, n + 1 + c)
                    dve.tensor_tensor_scan(state[:, c], decay[:, c], state[:, c], 0.0, ALU.mult,
                                           ALU.add).then_inc(scanned, 1)

                def gated_chunk(c):
                    dve.wait_ge(scanned, 3 * n + 1 + c)
                    if c == 0:
                        dve.wait_ge(gate_ready, 3 * n + 3)
                    dve.tensor_tensor(state[:, c], state[:, c], gate[:, p, c], ALU.mult).then_inc(y_ready, 1)

                def low_chunk(c):
                    dve.wait_ge(y_hi, n + 1 + c)
                    dve.tensor_tensor(y_l[:, c], state[:, c], raw(y_h[:, c]), ALU.subtract).then_inc(y_lo, 1)

                input_chunk(0)
                input_chunk(1)
                scale_chunk(0)
                scale_chunk(1)
                scan_chunk(0)
                input_chunk(2)
                gated_chunk(0)
                scan_chunk(1)
                scale_chunk(2)
                gated_chunk(1)
                scan_chunk(2)
                low_chunk(0)
                gated_chunk(2)
                low_chunk(1)
                low_chunk(2)
                ffn_low(n - 1, 2)
                add_att(n, p)
                ffn_low(n - 1, 3)
                norm(n, p, 1, xn2, xn2_ready, t2_done)

            def body(i, p):
                if at(i, 0):
                    return first(i, p)
                if at(i, NSEQ - 1):
                    return last(i, p)
                input_term(i)
                if at(i, 1):
                    add_att(0, 0)
                    norm(0, 0, 1, xn2, xn2_ready, t2_done)
                    dve.wait_ge(xn2_ready, NT)
                    add_tok(2, 0, (0, 1))
                    xb_low(0)
                    add_tok(2, 0, (2,))
                else:
                    xb_low(i - 1)
                    add_tok(i + 1, 1 - p)
                moments(i + 1, 0)
                scale_input(i, 0, 2)
                norm(i + 1, 1 - p, 0, xn1, xn1_ready, t1_done)
                scale_input(i, 2, 3)
                recur(i, range(0, 1))
                xa_low(i + 1, BANK_T1)
                recur(i, range(1, KH))
                gated(i, p)
                y_low(i)
                ffn_low(i - 1, 0)
                conv(i + 1, (1,))
                ffn_low(i - 1, 1)
                conv(i + 1, (2, 3))
                u_low(i + 1)
                add_att(i, p)
                norm(i, p, 1, xn2, xn2_ready, t2_done)
                scale_ffn(i - 1)

            steps(dve, body)
            n = NSEQ - 1
            p = n % 2
            xb_low(n, BANK_T2_LAST)
            scale_ffn(n - 1)
            for part in range(len(parts(n))):
                if part in (1, 2):
                    a, b = parts(n)[part]
                    dve.wait_ge(g_ready, 8 * n + b)
                    dve.wait_ge(ffn_done, n)
                    dve.tensor_copy(g_h[:, a:b], g[:, a:b]).then_inc(g_hi_last, 1)
                ffn_low(n, part)
            dve.wait_ge(outb_ready, n + 1)
            dve.wait_ge(out_ready, n)
            for t in range(NT):
                dve.wait_ge(ffn_done, n + 1 + t)
                dve.tensor_tensor(ffn_s[0:TT, t], ffn_tile(n, t), alpha2[0:TT, :],
                                  ALU.mult).then_inc(ffn_scaled, 1)
                dve.wait_ge(ffn_scaled, n + 1 + t)
                dve.tensor_tensor(outb[0:TT, p, t], outb[0:TT, p, t], ffn_s[0:TT, t], ALU.add).then_inc(out_ready, 1)

        @block.tensor
        def _(pe):
            def split_product(acc, pairs, first=True, last=True):
                for k, (a, b) in enumerate(pairs):
                    ins = pe.matmul(acc, a, b, start=(first and k == 0), stop=(last and k == len(pairs) - 1))
                return ins

            def busy(bank, n):
                for _ in range(n):
                    pe.matmul(ps[:, bank, 0:P], ones[:, :], ones[:, :], start=True, stop=True)

            def A_first():
                def add(t, j, which):
                    f0 = t * TT + SHIFTS[j // KX]
                    xh, xl = (x[:, j % KX, f0:f0 + TT] for x in (x_h, x_l))
                    pairs = [(xh, tok_wh[:, j]), (xh, tok_wl[:, j]), (xl, tok_wh[:, j])]
                    return split_product(ps[0:TT, BANK_TOK[t], 0:DIM], [pairs[w] for w in which],
                                         j == 0 and 0 in which, j == NJ - 1 and 2 in which)

                pe.wait_ge(x_hi, 1)
                pe.wait_ge(w_hi, 1)
                for t in range(NT):
                    for j in range(NJ // 2):
                        add(t, j, (0,))
                pe.wait_ge(w_lo, 1)
                for t in range(NT):
                    for j in range(NJ // 2):
                        add(t, j, (1,))
                pe.wait_ge(x_split, 1)
                for t in range(NT):
                    for j in range(NJ // 2):
                        add(t, j, (2,))
                pe.wait_ge(w_lo, 2)
                for t in range(NT):
                    for j in range(NJ // 2, NJ):
                        ins = add(t, j, (0, 1, 2))
                    ins.then_inc(tok_done, 1)

            def A(n, tiles=range(NT)):
                if at(n, 0):
                    return A_first()
                pe.wait_ge(x_split, n + 1)
                xs = (x1_h, x1_l) if at(n, 1) else (x_h, x_l)
                for t in tiles:
                    if at(n, 1):
                        pe.wait_ge(h_ready, t + 1)
                    else:
                        need(pe, tanh_ready, 6 * (n - 1) + t + (3 if at(n, 2) else 1))
                    for j in range(NJ):
                        f0 = t * TT + SHIFTS[j // KX]
                        xh, xl = (x[:, j % KX, f0:f0 + TT] for x in xs)
                        ins = split_product(ps[0:TT, BANK_TOK[t], 0:DIM],
                                            [(xh, tok_wh[:, j]), (xh, tok_wl[:, j]), (xl, tok_wh[:, j])],
                                            j == 0, j == NJ - 1)
                    ins.then_inc(tok_done, 1)

            def transposes(n, xn, ready, banks, done):
                for t in range(NT):
                    pe.wait_ge(ready, 3 * n + t + 1)
                    for c in range(KX):
                        ins = pe.transpose(ps[:, banks[c], t * TT:(t + 1) * TT], xn[0:TT, t, c * P:(c + 1) * P],
                                           ident[0:TT, 0:TT])
                        if t == NT - 1:
                            ins.then_inc(done, 1)

            def B(n, prev):
                for m in range(2 * KH):
                    held = {2: 5, 3: 3, 4: 4, 5: 2}
                    if exists(prev) and m in held:
                        pe.wait_ge(g_ready, 8 * prev + held[m] + 1)
                    if at(n, 0) and m < KH:
                        pe.wait_ge(h_ready, NT + m + 1)
                    if at(n, 1) and m in (0, 1, 2, 5):
                        pe.wait_ge(tanh_ready, 6 if m == 5 else m + 3)
                    bank = BANK_U[m] if m < KH else BANK_GATE[m - KH]
                    f0 = HID + m * P if m < KH else (m - KH) * P
                    for k in range(KX):
                        wh, wl = wi_h[:, k, f0:f0 + P], wi_l[:, k, f0:f0 + P]
                        if m == 0:
                            pe.wait_ge(xa_lo, 2 * n + k + 1)
                        ins = split_product(ps[:, bank, 0:TP], [(wh, xa_h[:, k]), (wl, xa_h[:, k]), (wh, xa_l[:, k])],
                                            k == 0, k == KX - 1)
                    ins.then_inc(gi_done, 1)

            def gate_part(n, m, k):
                wh, wl = wg_h[:, k, m * P:(m + 1) * P], wg_l[:, k, m * P:(m + 1) * P]
                return split_product(ps[:, fg_banks(n)[m], 0:TP], [(wh, u_h[:, k]), (wl, u_h[:, k]), (wh, u_l[:, k])],
                                     k == 0, k == KH - 1)

            def C_forget(n):
                if at(n, 0) or at(n, 1):
                    for k in range(KH):
                        pe.wait_ge(u_lo, 3 * n + k + 1)
                        for m in range(KH):
                            if k == KH - 1:
                                gate_part(n, m, k).then_inc(fg_done, 1)
                            else:
                                gate_part(n, m, k)
                    return
                for m in range(KH):
                    for k in range(KH):
                        if m == 0:
                            pe.wait_ge(u_lo, 3 * n + k + 1)
                        ins = gate_part(n, m, k)
                    ins.then_inc(fg_done, 1)

            def C_input(n, ms=range(KH, 2 * KH)):
                for m in ms:
                    if at(n, 0) or at(n, 1):
                        if m == 2 * KH - 1:
                            pe.wait_ge(gate_ready, 3 * n + 1)
                    else:
                        pe.wait_ge(h2_ready, 3 * (n - 1) + (m - KH) + 1)
                    for k in range(KH):
                        ins = gate_part(n, m, k)
                    ins.then_inc(fg_done, 1)

            def D(n, prev):
                banks = BANK_ATT_LAST if at(n, NSEQ - 1) else BANK_ATT
                for t in range(NT):
                    if at(n, 0):
                        pe.wait_ge(tanh_ready, 6 + (1, 2, 6)[t])
                    elif at(n, NSEQ - 1):
                        pe.wait_ge(g_ready, 8 * prev + t + 1)
                        if t == 0:
                            busy(banks[0], KEEP_WARM)
                    elif t < 2:
                        pe.wait_ge(g_ready, 8 * prev + 7 + t)
                    else:
                        pe.wait_ge(gate_ready, 3 * (n + 1) + 1)
                    for k in range(KH):
                        if t == 0 and (k == 0 or at(n, NSEQ - 1)):
                            pe.wait_ge(y_lo, n + 1 + k)
                        yh, yl = (y[:, k, t * TT:(t + 1) * TT] for y in (y_h, y_l))
                        ins = split_product(ps[0:TT, banks[t], 0:DIM],
                                            [(yh, wo_h[:, k]), (yh, wo_l[:, k]), (yl, wo_h[:, k])],
                                            k == 0, k == KH - 1)
                    ins.then_inc(att_done, 1)

            def E(n, half):
                for c in range(*parts(n)[half]):
                    if at(n, NSEQ - 2):
                        held = {0: 1, 1: 2, 2: 3, 5: 4, 6: 5, 7: 6}
                        if c in held:
                            pe.wait_ge(tanh_ready, 6 * (n + 1) + held[c])
                    elif c < 3 and exists(n + 1):
                        pe.wait_ge(tanh_ready, 6 * (n + 1) + 4 + c)
                    if at(n, NSEQ - 1) and c == 3:
                        pe.wait_ge(ffn_scaled, n)
                    if c == 5 and exists(n + 2):
                        pe.wait_ge(h_ready, 3 * (n + 2) + 3)
                    if c >= 6 and not at(n, NSEQ - 2):
                        pe.wait_ge(g_ready, 8 * n + c - 5)
                    for k in range(KX):
                        if c == 0:
                            pe.wait_ge(xb_lo, 2 * n + k + 1)
                        w = w1_sign[:, k, c * P:(c + 1) * P]
                        ins = split_product(ps[:, e_banks(n)[c], 0:TP], [(w, xb_h[:, k]), (w, xb_l[:, k])],
                                            k == 0, k == KX - 1)
                    ins.then_inc(ff1_done, 1)

            def ffn_pairs(t, a, b):
                return [(gp[:, c, t * TT:(t + 1) * TT], w2_sign[:, c]) for c in range(a, b) for gp in (g_h, g_l)]

            def F(n):
                if exists(n + 2):
                    pe.wait_ge(gate_ready, 3 * (n + 2) + 3)
                for k, (a, b) in enumerate(parts(n)):
                    pe.wait_ge(g_lo, 2 * n + k + 1)
                    for t in (0, 2):
                        split_product(ffn_tile(n, t), ffn_pairs(t, a, b), a == 0, b == KF)
                split_product(ffn_tile(n, 1), ffn_pairs(1, 0, KF)).then_inc(ffn_done, 1)

            def F_last(n, ks):
                for k in ks:
                    a, b = parts(n)[k]
                    if at(n, NSEQ - 1) and k >= 2:
                        continue
                    if at(n, NSEQ - 1):
                        pe.wait_ge(g_lo, 2 * n + k + 1)
                    elif k < 2:
                        pe.wait_ge(g_lo_pool, k + 1)
                    else:
                        pe.wait_ge(g_lo, 2 * n + k - 1)
                    for t in range(NT):
                        if k == 0 and (at(n, NSEQ - 2) or t == 2):
                            pe.wait_ge(g_ready, 8 * n + (4 + t if at(n, NSEQ - 2) else 3))
                        ins = split_product(ffn_tile(n, t), ffn_pairs(t, a, b), a == 0, b == KF)
                    if b == KF:
                        ins.then_inc(ffn_done, 1)
                if at(n, NSEQ - 1):
                    for t in range(NT):
                        for k in (2, 3):
                            if t == 0:
                                pe.wait_ge(g_lo, 2 * n + k + 1)
                            ins = split_product(ffn_tile(n, t), ffn_pairs(t, *parts(n)[k]), False, k == 3)
                        ins.then_inc(ffn_done, 1)

            pe.wait_ge(consts_ready, 1)
            busy(BANK_FFN, WARM_UP)
            A(0)
            A(1, (0, 1))
            pe.wait_ge(ident_ready, 1)
            transposes(0, xn1, xn1_ready, BANK_T1_FIRST, t1_done)
            A(1, (2,))
            pe.wait_ge(wi_lo, 1)
            pe.wait_ge(pads_ready, 4)
            B(0, -1)
            pe.wait_ge(wg_lo, KH)
            pe.wait_ge(pads_ready, 6)

            def body(i, p):
                if at(i, 0):
                    C_forget(0)
                    pe.wait_ge(gate_ready, 3)
                    transposes(1, xn1, xn1_ready, BANK_T1_SECOND, t1_done)
                    C_input(0)
                    B(1, -1)
                    return
                if at(i, NSEQ - 1):
                    C_forget(i)
                    C_input(i, [KH])
                    pe.wait_ge(ffn_scaled, i - 1)
                    transposes(i - 1, xn2, xn2_ready, BANK_T2, t2_done)
                    C_input(i, [KH + 1, KH + 2])
                    for part in range(len(parts(i - 1))):
                        E(i - 1, part)
                    D(i, i - 1)
                    F_last(i - 1, range(0, 3))
                    transposes(i, xn2, xn2_ready, BANK_T2_LAST, t2_done)
                    F_last(i - 1, range(3, 4))
                    return
                C_forget(i)
                C_input(i)
                if at(i, 1):
                    pe.wait_ge(consts_ready, 3)
                    pe.wait_ge(folded, 4)
                    pe.wait_ge(gate_ready, 6)
                    for c in range(KF):
                        ins = pe.matmul(ps[:, BANK_ALPHA[0], 2 * c:2 * c + 2], stage_a[:, c * P:(c + 1) * P],
                                        ones[:, 0:2], start=True, stop=True)
                    ins.then_inc(alpha_sum, 1)
                    pe.matmul(ps[:, BANK_ALPHA[1], 0:DIM], ones[:, :], stage_b[:, 0:DIM], start=True,
                              stop=True).then_inc(alpha_sum, 1)
                    pe.wait_ge(w_lo, 3)
                    D(0, -1)
                    A(2)
                    pe.wait_ge(alpha_ready, 2)
                    transposes(0, xn2, xn2_ready, BANK_T2, t2_done)
                else:
                    pe.wait_ge(ffn_scaled, i - 1)
                    transposes(i - 1, xn2, xn2_ready, BANK_T2, t2_done)
                    A(i + 1)
                E(i - 1, 0)
                transposes(i + 1, xn1, xn1_ready, BANK_T1, t1_done)
                E(i - 1, 1)
                B(i + 1, i - 1)
                D(i, i - 1)
                F(i - 1)

            steps(pe, body)
            n = NSEQ - 1
            for part in range(len(parts(n))):
                E(n, part)
            F_last(n, range(0, 4))


def chunked(a, k):
    import numpy as np
    return np.ascontiguousarray(a.reshape(k, P, a.shape[1]).transpose(1, 0, 2).reshape(P, k * a.shape[1]))


def kernel(x, L0_tok_W, L0_tok_b, L0_attn_Wi, L0_attn_conv_w, L0_attn_conv_b, L0_attn_Wg, L0_attn_bg,
           L0_attn_forget_base, L0_attn_Wo, L0_ffn_w1, L0_ffn_b1, L0_ffn_w2, L0_ffn_b2):
    import numpy as np
    import concourse.bacc as bacc
    from concourse.bass_utils import run_bass_kernel_spmd

    def cols(v):
        return np.asarray(v).reshape(-1, P).T

    conv_w = np.asarray(L0_attn_conv_w).reshape(KH, P, TAPS).transpose(1, 0, 2).reshape(P, KH * TAPS)
    arrays = {
        "xT": np.ascontiguousarray(np.asarray(x).reshape(NSEQ, T_IN, KX, P).transpose(0, 3, 2, 1)),
        "wtokT": chunked(np.asarray(L0_tok_W).T, NJ),
        "wiT": chunked(np.asarray(L0_attn_Wi).T, KX),
        "wgT": chunked(np.asarray(L0_attn_Wg).T, KH),
        "woT": chunked(np.asarray(L0_attn_Wo).T, KH),
        "w1T": chunked(np.asarray(L0_ffn_w1).T, KX),
        "w2T": chunked(np.asarray(L0_ffn_w2).T, KF),
        "params": np.ascontiguousarray(np.concatenate(
            [conv_w, cols(L0_attn_conv_b), cols(L0_attn_bg), cols(L0_attn_forget_base), cols(L0_ffn_b1)], axis=1)),
        "rows": np.ascontiguousarray(np.stack([np.asarray(L0_tok_b), np.asarray(L0_ffn_b2)])),
    }
    nc = bacc.Bacc("TRN2", target_bir_lowering=False, num_devices=1)
    args = [nc.dram_tensor(name, a.shape, F32, kind="ExternalInput").ap() for name, a in arrays.items()]
    out = nc.dram_tensor("out", (NSEQ, T, DIM), F32, kind="ExternalOutput").ap()
    tower(nc, *args, out.rearrange("s (t p) d -> s p t d", p=TT))
    r = run_bass_kernel_spmd(nc, [arrays], core_ids=[0])
    return r.results[0]["out"]
```
